# Optimizing a Trainium2 kernel written in Bass

```python
import numpy as np
import jax
import jax.numpy as jnp

def _softmax(x, axis=-1):
    return jax.nn.softmax(x, axis=axis)

def _gelu(x):
    return jax.nn.gelu(x, approximate=True)

def _silu(x):
    return jax.nn.silu(x)

def _sigmoid(x):
    return jax.nn.sigmoid(x)

def _layernorm(x, axis=-1, eps=1e-05):
    m = jnp.mean(x, axis=axis, keepdims=True)
    v = jnp.var(x, axis=axis, keepdims=True)
    return (x - m) / jnp.sqrt(v + eps)

def _scatter_add(tgt, idx, src, axis=0):
    return tgt.at[idx].add(src)

def _segment_sum(src, seg, n):
    return jax.ops.segment_sum(src, seg, n)
kernel_name = 'mk_cond_seq_d1_seqx_r2_fb3a59'

def setup_inputs(seed: int=0):
    np.random.seed(seed)
    _w = jnp.asarray

    def _rec_inputs():
        import jax
        import jax.numpy as jnp
        _rk = jax.random.key(seed)
        x = 7.22e-05 + 1 * jax.random.normal(jax.random.fold_in(_rk, 1), (4, 1024, 512), jnp.float32)
        _lenS = 1024 - jax.random.randint(jax.random.fold_in(_rk, 7), (4,), 0, max(1, 1024 // 4) + 1, jnp.int32)
        _lenS2 = 1024 - jax.random.randint(jax.random.fold_in(_rk, 8), (4,), 0, max(1, 1024 // 4) + 1, jnp.int32)
        cond_1024 = 0.00782532 + 1.00527 * jax.random.normal(jax.random.fold_in(_rk, 11), (4, 512), jnp.float32)
        _validS = jnp.arange(1024)[None, :] < _lenS[:, None]
        _validS2 = jnp.arange(1024)[None, :] < _lenS2[:, None]
        _causal = jnp.tril(jnp.ones((1024, 1024), dtype=bool))
        mask_BxS_bk1 = jnp.broadcast_to(_validS[:, :], (4, 1024))
        return (x, cond_1024, mask_BxS_bk1)
    x, cond_1024, mask_BxS_bk1 = _rec_inputs()

    def _L0_cond_setup():
        import jax, jax.numpy as jnp
        import numpy as np
        B, N, C = (8, 512, 512)
        H = 16
        HD = C // H
        MLP = 4 * C
        EPS = 1e-06

        def _layernorm(x):
            mu = jnp.mean(x, axis=-1, keepdims=True)
            var = jnp.mean((x - mu) ** 2, axis=-1, keepdims=True)
            return (x - mu) * jax.lax.rsqrt(var + EPS)

        def _modulate(x, shift, scale):
            return x * (1.0 + scale[:, None, :]) + shift[:, None, :]

        def _attention(x, padding_mask, qkv_w, qkv_b, proj_w, proj_b):
            b, n, cdim = x.shape
            qkv = x @ qkv_w.T + qkv_b
            qkv = qkv.reshape(b, n, 3, H, HD).transpose(2, 0, 3, 1, 4)
            q, k, v = (qkv[0], qkv[1], qkv[2])
            scale = HD ** (-0.5)
            attn = jnp.einsum('bhnd,bhmd->bhnm', q, k) * scale
            mask = padding_mask[:, None, :] & padding_mask[:, :, None]
            attn = jnp.where(mask[:, None, :, :], attn, -1000000000.0)
            attn = jax.nn.softmax(attn, axis=-1)
            out = jnp.einsum('bhnm,bhmd->bhnd', attn, v)
            out = out.transpose(0, 2, 1, 3).reshape(b, n, cdim)
            return out @ proj_w.T + proj_b
        key = jax.random.key(seed)
        ks = jax.random.split(key, 12)
        x = jax.random.normal(ks[0], (B, N, C), dtype=jnp.float32)
        c = jax.random.normal(ks[1], (B, C), dtype=jnp.float32)
        lengths = jax.random.randint(ks[2], (B,), N // 2, N + 1)
        padding_mask = jnp.arange(N)[None, :] < lengths[:, None]
        s = 0.02
        qkv_w = jax.random.normal(ks[3], (3 * C, C), dtype=jnp.float32) * s
        qkv_b = jnp.zeros((3 * C,), dtype=jnp.float32)
        proj_w = jax.random.normal(ks[4], (C, C), dtype=jnp.float32) * s
        proj_b = jnp.zeros((C,), dtype=jnp.float32)
        fc1_w = jax.random.normal(ks[5], (MLP, C), dtype=jnp.float32) * s
        fc1_b = jnp.zeros((MLP,), dtype=jnp.float32)
        fc2_w = jax.random.normal(ks[6], (C, MLP), dtype=jnp.float32) * s
        fc2_b = jnp.zeros((C,), dtype=jnp.float32)
        ada_w = jax.random.normal(ks[7], (6 * C, C), dtype=jnp.float32) * s
        ada_b = jnp.zeros((6 * C,), dtype=jnp.float32)
        return {'x': x, 'c': c, 'padding_mask': padding_mask, 'qkv_w': qkv_w, 'qkv_b': qkv_b, 'proj_w': proj_w, 'proj_b': proj_b, 'fc1_w': fc1_w, 'fc1_b': fc1_b, 'fc2_w': fc2_w, 'fc2_b': fc2_b, 'ada_w': ada_w, 'ada_b': ada_b}
    _L0_cond_all = _L0_cond_setup()
    _L0_cond_in = {k: v for k, v in _L0_cond_all.items() if k in ('qkv_w', 'qkv_b', 'proj_w', 'proj_b', 'fc1_w', 'fc1_b', 'fc2_w', 'fc2_b', 'ada_w', 'ada_b')}
    del _L0_cond_all
    return {'x': x, 'cond_1024': cond_1024, 'mask_BxS_bk1': mask_BxS_bk1, 'L0_cond_qkv_w': _L0_cond_in['qkv_w'], 'L0_cond_qkv_b': _L0_cond_in['qkv_b'], 'L0_cond_proj_w': _L0_cond_in['proj_w'], 'L0_cond_proj_b': _L0_cond_in['proj_b'], 'L0_cond_fc1_w': _L0_cond_in['fc1_w'], 'L0_cond_fc1_b': _L0_cond_in['fc1_b'], 'L0_cond_fc2_w': _L0_cond_in['fc2_w'], 'L0_cond_fc2_b': _L0_cond_in['fc2_b'], 'L0_cond_ada_w': _L0_cond_in['ada_w'], 'L0_cond_ada_b': _L0_cond_in['ada_b']}

def reference(x, cond_1024, mask_BxS_bk1, L0_cond_qkv_w, L0_cond_qkv_b, L0_cond_proj_w, L0_cond_proj_b, L0_cond_fc1_w, L0_cond_fc1_b, L0_cond_fc2_w, L0_cond_fc2_b, L0_cond_ada_w, L0_cond_ada_b):
    import jax
    import jax.numpy as jnp

    def _L0_cond_ref(x, c, padding_mask, qkv_w, qkv_b, proj_w, proj_b, fc1_w, fc1_b, fc2_w, fc2_b, ada_w, ada_b):
        import jax, jax.numpy as jnp
        import numpy as np
        B, N, C = (8, 512, 512)
        H = 16
        HD = C // H
        MLP = 4 * C
        EPS = 1e-06

        def _layernorm(x):
            mu = jnp.mean(x, axis=-1, keepdims=True)
            var = jnp.mean((x - mu) ** 2, axis=-1, keepdims=True)
            return (x - mu) * jax.lax.rsqrt(var + EPS)

        def _modulate(x, shift, scale):
            return x * (1.0 + scale[:, None, :]) + shift[:, None, :]

        def _attention(x, padding_mask, qkv_w, qkv_b, proj_w, proj_b):
            b, n, cdim = x.shape
            qkv = x @ qkv_w.T + qkv_b
            qkv = qkv.reshape(b, n, 3, H, HD).transpose(2, 0, 3, 1, 4)
            q, k, v = (qkv[0], qkv[1], qkv[2])
            scale = HD ** (-0.5)
            attn = jnp.einsum('bhnd,bhmd->bhnm', q, k) * scale
            mask = padding_mask[:, None, :] & padding_mask[:, :, None]
            attn = jnp.where(mask[:, None, :, :], attn, -1000000000.0)
            attn = jax.nn.softmax(attn, axis=-1)
            out = jnp.einsum('bhnm,bhmd->bhnd', attn, v)
            out = out.transpose(0, 2, 1, 3).reshape(b, n, cdim)
            return out @ proj_w.T + proj_b
        mod = jax.nn.silu(c) @ ada_w.T + ada_b
        shift_msa, scale_msa, gate_msa, shift_mlp, scale_mlp, gate_mlp = jnp.split(mod, 6, axis=1)
        h = _modulate(_layernorm(x), shift_msa, scale_msa)
        x = x + gate_msa[:, None, :] * _attention(h, padding_mask, qkv_w, qkv_b, proj_w, proj_b)
        h = _modulate(_layernorm(x), shift_mlp, scale_mlp)
        h = jax.nn.gelu(h @ fc1_w.T + fc1_b, approximate=True) @ fc2_w.T + fc2_b
        x = x + gate_mlp[:, None, :] * h
        return x
    x = _L0_cond_ref(x, cond_1024, mask_BxS_bk1, L0_cond_qkv_w, L0_cond_qkv_b, L0_cond_proj_w, L0_cond_proj_b, L0_cond_fc1_w, L0_cond_fc1_b, L0_cond_fc2_w, L0_cond_fc2_b, L0_cond_ada_w, L0_cond_ada_b)
    return x

_drawn_inputs = setup_inputs


def setup_inputs(seed=0):
    import zlib

    import numpy as np

    out = dict(_drawn_inputs(seed))
    spreads = {'L0_cond_qkv_b': (0.0, 0.673),
     'L0_cond_proj_b': (0.0, 0.276),
     'L0_cond_fc1_b': (0.0, 0.539),
     'L0_cond_fc2_b': (0.0, 0.283),
     'L0_cond_ada_b': (0.0, 0.1)}
    factors = {'L0_cond_qkv_w': 3.573, 'L0_cond_proj_w': 2.696}
    for name, (base, spread) in spreads.items():
        noise = np.random.default_rng([zlib.crc32(name.encode()), seed]).standard_normal(out[name].shape)
        drawn = base * np.exp(spread * noise) if base else spread * noise
        out[name] = jnp.asarray(drawn.astype(out[name].dtype))
    for name, factor in factors.items():
        out[name] = (out[name] * factor).astype(out[name].dtype)
    return out
```

```python
from contextlib import ExitStack

import concourse.bass as bass
from concourse import mybir

F32 = mybir.dt.float32
F32R = mybir.dt.float32r
U8 = mybir.dt.uint8
ALU = mybir.AluOpType
ACT = mybir.ActivationFunctionType
AX_X = mybir.AxisListType.X

B, S, C = 4, 1024, 512
HEADS, HD, HIDDEN = 16, 32, 2048
EPS = 1e-6
P = 128
KT = C // P
TT = S // P
G = C // P
HG = HEADS // G
JT = HIDDEN // G // P
N = 512
HALVES = S // N
TILES = HG * TT
STACK = 3 * HD
MASK_ROW = STACK
MAX_ROW = STACK + 1
SCALE = HD ** -0.5
NEG = 1.0e9
QKV_W = 3 * KT * P
FC1_W = KT * JT * P
FC2_W = JT * C
NMOD = 4 * KT
FC2_FIRST = 10


def fc2_schedule():
    return {FC2_FIRST + (tt * (TILES - FC2_FIRST)) // (TT - 1): tt for tt in range(TT - 1)}


def block_kernel(nc, x, cond_t, mask, wqkv, wproj, wfc1, wfc2, proj_b, fc2_b, ada_wt, ada_bt, ada_bg, out):
    x1_dram = nc.dram_tensor("x1_dram", (B, S, C), F32, kind="Internal").ap()
    gate_dram = nc.dram_tensor("gate_dram", (B, 2 * C), F32, kind="Internal").ap()
    fc2_at = fc2_schedule()

    with ExitStack() as ctx:
        def sb(name, shape, dt=F32):
            return ctx.enter_context(nc.sbuf_tensor(name, shape, dt))

        def sem(name):
            return ctx.enter_context(nc.semaphore(name))

        w_qkv = sb("w_qkv", [P, QKV_W + 3])
        w_proj = sb("w_proj", [P, C])
        w_raw = sb("w_raw", [P, FC1_W + JT])
        w_hi = sb("w_hi", [P, FC1_W], F32R)
        w_lo = sb("w_lo", [P, FC1_W], F32R)
        fc1_bias = sb("fc1_bias", [P, JT])
        attn_acc = sb("attn_acc", [P, TT, C])
        mlp_acc = sb("mlp_acc", [P, TT, C])
        h1 = sb("h1", [P, KT, S])
        h2_hi = sb("h2_hi", [P, KT, S], F32R)
        h2_lo = sb("h2_lo", [P, KT, S], F32R)
        q_st = sb("q_st", [P, HG, S], F32R)
        k_st = sb("k_st", [P, HG, S], F32R)
        v_tok = sb("v_tok", [P, TT, P])
        q_mask = sb("q_mask", [P, S])
        mask_u8 = sb("mask_u8", [P, S], U8)
        gate1 = sb("gate1", [P, C])
        gate2 = sb("gate2", [P, C])
        den_row = sb("den_row", [HG, S])
        ident = sb("ident", [P, P])
        head_sel = sb("head_sel", [HG, P])
        neg_max = sb("neg_max", [P, TILES])
        den = sb("den", [P, TILES])
        stat = sb("stat", [P, 3 * TILES])
        stat_t = sb("stat_t", [3 * TILES, P])
        mod_all = sb("mod_all", [P, B, NMOD])
        mod = sb("mod", [P, NMOD])
        eps_col = sb("eps_col", [P, 1])
        bn6 = sb("bn6", [P, TT, 6])
        mean_var = sb("mean_var", [P, TT, 2])
        std = sb("std", [P, TT])
        rstd = sb("rstd", [P, TT])
        shift = sb("shift", [P, TT])
        ada_bias = sb("ada_bias", [P, NMOD])
        cond = sb("cond", [P, KT * B])
        silu = sb("silu", [P, KT * B])

        def in_turn(*layouts):
            made = []
            for layout in layouts:
                with ExitStack() as turn:
                    made.append([turn.enter_context(nc.sbuf_tensor(n, s, d)) for n, s, d in layout])
            return made

        big = in_turn(
            [("u_hi", [P, JT, S], F32R), ("u_lo", [P, JT, S], F32R)],
            [("probs", [P, 2 * HG, S], F32)],
            [("qf", [P, S], F32), ("kf", [P, S], F32), ("q_hi", [P, S], F32R), ("q_lo", [P, S], F32R),
             ("k_hi", [P, S], F32R), ("k_lo", [P, S], F32R), ("v_ch", [P, S], F32)],
            [("x_tiles", [P, TT, C], F32), ("x_more", [P, TT, C], F32)],
            [("ada_w", [P, 4, KT, C], F32)],
        )
        (u_hi, u_lo), (probs,), (qf, kf, q_hi, q_lo, k_hi, k_lo, v_ch), (x_tiles, x_more), (ada_w,) = big
        ctx.enter_context(nc.sbuf_tensor("big_region", [P, 2 * HG * S], F32))
        (gate_bias, gate_rows), (u_full,), (attn_ch, den_bc) = in_turn(
            [("gate_bias", [B, 2 * C], F32), ("gate_rows", [B, 2 * C], F32)],
            [("u_full", [P, 4, N], F32)],
            [("attn_ch", [P, S], F32), ("den_bc", [P, S], F32)],
        )
        ctx.enter_context(nc.sbuf_tensor("small_region", [P, 2 * S], F32))

        pair = [ctx.enter_context(nc.psum_tensor(f"pair{i}", [P, S], F32)) for i in range(3)]
        tail = ctx.enter_context(nc.psum_tensor("tail", [P, S], F32))

        consts_ready = sem("consts_ready")
        ident_zero = sem("ident_zero")
        stacks_primed = sem("stacks_primed")
        small_loaded = sem("small_loaded")
        ada_loaded = [sem(f"ada_loaded{i}") for i in range(6)]
        silu_step = sem("silu_step")
        silu_exp = sem("silu_exp")
        silu_ready = sem("silu_ready")
        ada_done = sem("ada_done")
        gates_ready = sem("gates_ready")
        mod_step = sem("mod_step")
        gates_stored = sem("gates_stored")
        x_loaded = sem("x_loaded")
        mask_loaded = sem("mask_loaded")
        mask_ready = sem("mask_ready")
        mask_rows = sem("mask_rows")
        mod_ready = sem("mod_ready")
        acc_loaded = sem("acc_loaded")
        var_ready = [sem("var1_ready"), sem("var2_ready")]
        std_ready = [sem("std1_ready"), sem("std2_ready")]
        norm_ready = [sem("norm1_ready"), sem("norm2_ready")]
        norm_t = [sem("norm1_t"), sem("norm2_t")]
        even_out = [sem("even1_out"), sem("even2_out")]
        odd_out = [sem("odd1_out"), sem("odd2_out")]
        norm_step = sem("norm_step")
        gated = sem("gated")
        h2_split = sem("h2_split")
        h2_ready = sem("h2_ready")
        gates_loaded = sem("gates_loaded")
        x_again = sem("x_again")
        x1_ready = sem("x1_ready")
        x1_stored = sem("x1_stored")
        x1_again = sem("x1_again")
        final_ready = sem("final_ready")
        out_stored = sem("out_stored")
        mlp_acc_loaded = sem("mlp_acc_loaded")
        wqkv_loaded = sem("wqkv_loaded")
        wproj_loaded = sem("wproj_loaded")
        qkv_full = sem("qkv_full")
        q_full_ready = sem("q_full_ready")
        k_full_ready = sem("k_full_ready")
        q_hi_ready = sem("q_hi_ready")
        k_hi_ready = sem("k_hi_ready")
        q_lo_ready = sem("q_lo_ready")
        k_lo_ready = sem("k_lo_ready")
        v_ch_ready = sem("v_ch_ready")
        v_t = sem("v_t")
        v_ready = sem("v_ready")
        stack_loaded = sem("stack_loaded")
        score_full = sem("score_full")
        neg_max_ready = sem("neg_max_ready")
        den_ready = sem("den_ready")
        stat_step = sem("stat_step")
        stat_ready = sem("stat_ready")
        stat_turned = sem("stat_turned")
        stat_t_ready = sem("stat_t_ready")
        rows_loaded = sem("rows_loaded")
        score_t_full = sem("score_t_full")
        probs_ready = sem("probs_ready")
        probs_used = sem("probs_used")
        den_spread = sem("den_spread")
        den_bc_ready = sem("den_bc_ready")
        attn_ready = sem("attn_ready")
        proj_full = sem("proj_full")
        proj_added = sem("proj_added")
        raw_loaded = sem("raw_loaded")
        w_hi_ready = sem("w_hi_ready")
        w_ready = sem("w_ready")
        fc1_full = sem("fc1_full")
        gelu_ready = sem("gelu_ready")
        u_hi_ready = sem("u_hi_ready")
        u_ready = sem("u_ready")
        fc2_full = sem("fc2_full")
        fc2_added = sem("fc2_added")

        block = ctx.enter_context(nc.Block())

        def row_block(dram, b):
            return dram[bass.ds(b, 1)].rearrange("o (t p) c -> p (o t) c", p=P)

        def loops(eng, start, step, end):
            start(0)
            with eng.Fori(0, G) as g:
                step(g, g, None, 0)
            end(0, False)
            with eng.Fori(1, B) as b:
                start(b)
                with eng.Fori(0, G) as g:
                    step(b * G + g, g, b * G + g - G, b)
                end(b, True)
            with eng.Fori(0, G) as g:
                step(None, g, g + (B - 1) * G, B)

        @block.sync
        def _(sp):
            sp.dma_start(cond[:, :], cond_t).then_inc(small_loaded, 16)
            sp.dma_start(ada_bias[:, :], ada_bt).then_inc(small_loaded, 16)
            sp.dma_start(gate_bias[:, :], ada_bg.broadcast_to((B, 2 * C))).then_inc(small_loaded, 16)
            for i in range(6):
                if i >= 4:
                    sp.wait_ge(ada_done, i - 3)
                sp.dma_start(ada_w[:, i % 4], ada_wt[i]).then_inc(ada_loaded[i], 16)
            sp.dma_start(w_qkv[:, :], wqkv[0]).then_inc(wqkv_loaded, 16)
            sp.dma_start(w_proj[:, :], wproj[0]).then_inc(wproj_loaded, 16)
            sp.dma_start(w_raw[:, :], wfc1[0]).then_inc(raw_loaded, 16)
            sp.dma_start(mlp_acc[:, :, :], fc2_b.broadcast_to((P, TT, C))).then_inc(mlp_acc_loaded, 16)
            sp.wait_ge(gates_ready, 2)
            sp.dma_start(gate_dram, gate_rows[:, :]).then_inc(gates_stored, 16)
            sp.wait_ge(gates_stored, 16)

            def start(b):
                sp.wait_ge(ada_done, 6)
                sp.wait_ge(h2_ready, TT * b)
                sp.dma_start(attn_acc[:, :, :], proj_b.broadcast_to((P, TT, C))).then_inc(acc_loaded, 16)
                sp.dma_start(x_tiles[:, :, :], row_block(x, b)).then_inc(x_loaded, 16)
                sp.dma_start(mask_u8[:, :], mask[bass.ds(b, 1)].broadcast_to((P, S))).then_inc(mask_loaded, 16)

            def step(n, g, m, b):
                if m is not None:
                    sp.wait_ge(w_ready, 2 * m + 1)
                    sp.dma_start(w_raw[:, 0:FC2_W], wfc2[bass.ds(g, 1)].rearrange("o p c -> (o p) c")).then_inc(raw_loaded, 16)
                if n is not None:
                    for hi, lo, hi_ready, lo_ready, st, order in (
                            (q_hi, q_lo, q_hi_ready, q_lo_ready, q_st, "hhl"),
                            (k_hi, k_lo, k_hi_ready, k_lo_ready, k_st, "hlh")):
                        sp.wait_ge(hi_ready, n + 1)
                        for part in sorted(range(3), key=lambda i: order[i]):
                            if order[part] == "l":
                                sp.wait_ge(lo_ready, n + 1)
                            src = hi if order[part] == "h" else lo
                            for h in range(HG):
                                sp.dma_start(st[part * HD:(part + 1) * HD, h, :].bitcast(F32),
                                             src[h * HD:(h + 1) * HD, :].bitcast(F32)).then_inc(stack_loaded, 16)
                    sp.wait_ge(v_ch_ready, HALVES * (n + 1))
                    sp.dma_start(w_qkv[:, :], wqkv[bass.ds(g + 1, 1)].rearrange("o p c -> (o p) c")).then_inc(wqkv_loaded, 16)
                if m is not None:
                    sp.wait_ge(w_ready, 2 * m + 2)
                    sp.dma_start(w_raw[:, :], wfc1[bass.ds(g + 1, 1)].rearrange("o p c -> (o p) c")).then_inc(raw_loaded, 16)
                if n is not None:
                    sp.wait_ge(stat_t_ready, n + 1)
                    for r in range(2):
                        sp.dma_start(q_st[MAX_ROW + r:MAX_ROW + r + 1, :, :].bitcast(F32).rearrange("o h (t j) -> o (h t) j", j=P),
                                     stat_t[r * TILES:(r + 1) * TILES, :]).then_inc(rows_loaded, 16)
                    for h in range(HG):
                        sp.dma_start(den_row[h:h + 1, :].rearrange("o (t j) -> o t j", j=P),
                                     stat_t[2 * TILES + h * TT:2 * TILES + (h + 1) * TT, :]).then_inc(rows_loaded, 16)
                    sp.wait_ge(proj_full, TT * (n + 1))
                    sp.dma_start(w_proj[:, :], wproj[bass.ds(g + 1, 1)].rearrange("o p c -> (o p) c")).then_inc(wproj_loaded, 16)

            def finalize(f, more):
                sp.dma_start(x_more[:, :, :], row_block(x1_dram, f)).then_inc(x1_again, 16)
                sp.dma_start(gate2[:, :], gate_dram[bass.ds(f, 1), C:2 * C].broadcast_to((P, C))).then_inc(x1_again, 16)
                sp.wait_ge(final_ready, f + 1)
                sp.dma_start(row_block(out, f), x_more[:, :, :]).then_inc(out_stored, 16)
                if more:
                    sp.dma_start(mlp_acc[:, :, :], fc2_b.broadcast_to((P, TT, C))).then_inc(mlp_acc_loaded, 16)

            def end(b, with_mlp):
                sp.wait_ge(probs_used, TT * G * (b + 1))
                sp.dma_start(x_tiles[:, :, :], row_block(x, b)).then_inc(x_again, 16)
                sp.dma_start(gate1[:, :], gate_dram[bass.ds(b, 1), 0:C].broadcast_to((P, C))).then_inc(x_again, 16)
                if with_mlp:
                    finalize(b - 1, True)
                sp.wait_ge(x1_ready, b + 1)
                sp.dma_start(row_block(x1_dram, b), x_tiles[:, :, :]).then_inc(x1_stored, 16)

            loops(sp, start, step, end)
            sp.wait_ge(fc2_full, TT * G * B)
            sp.wait_ge(x1_stored, 16 * B)
            finalize(B - 1, False)
            sp.wait_ge(out_stored, 16 * B)
            sp.wait_ge(wqkv_loaded, 16 * (G * B + 1))
            sp.wait_ge(wproj_loaded, 16 * (G * B + 1))
            sp.wait_ge(raw_loaded, 16 * (2 * G * B + 1))

        @block.gpsimd
        def _(pool):
            nc.gpsimd.memset(ident[:, :], 0.0).then_inc(ident_zero, 1)
            nc.gpsimd.memset(head_sel[:, :], 1.0).then_inc(ident_zero, 1)
            nc.gpsimd.memset(eps_col[:, :], EPS).then_inc(ident_zero, 1)
            pool.wait_ge(ident_zero, 3)
            nc.gpsimd.affine_select(out=ident[:, :], in_=ident[:, :], compare_op=ALU.not_equal, fill=1.0,
                                    base=0, pattern=[[-1, P]], channel_multiplier=1).then_inc(consts_ready, 1)
            sel = head_sel[:, :].rearrange("p (h d) -> p h d", d=HD)
            nc.gpsimd.affine_select(out=sel, in_=sel, compare_op=ALU.is_equal, fill=0.0,
                                    base=0, pattern=[[-1, HG], [0, HD]], channel_multiplier=1).then_inc(consts_ready, 1)

            def start(b):
                pass

            def split_low(part, m):
                pool.wait_ge(w_hi_ready, 2 * m + part + 1)
                for c in range(FC2_W // N):
                    cols = slice(c * N, (c + 1) * N)
                    done = nc.gpsimd.tensor_tensor(w_lo[:, cols], w_raw[:, cols], w_hi[:, cols].bitcast(F32), ALU.subtract)
                done.then_inc(w_ready, 1)

            def step(n, g, m, b):
                if m is not None:
                    split_low(0, m)
                if n is not None:
                    pool.wait_ge(q_hi_ready, n + 1)
                    nc.gpsimd.tensor_tensor(q_lo[:, :], qf[:, :], q_hi[:, :].bitcast(F32), ALU.subtract).then_inc(q_lo_ready, 1)
                    pool.wait_ge(k_hi_ready, n + 1)
                    nc.gpsimd.tensor_tensor(k_lo[:, :], kf[:, :], k_hi[:, :].bitcast(F32), ALU.subtract).then_inc(k_lo_ready, 1)
                if m is not None:
                    for i in range(JT * HALVES):
                        j, half = i // HALVES, i % HALVES
                        cols = slice(half * N, (half + 1) * N)
                        pool.wait_ge(u_hi_ready, JT * HALVES * m + i + 1)
                        nc.gpsimd.tensor_tensor(u_lo[:, j, cols], u_full[:, i % 4, :], u_hi[:, j, cols].bitcast(F32),
                                                ALU.subtract).then_inc(u_ready, 1)
                    split_low(1, m)

            def end(b, with_mlp):
                for t in range(TT):
                    pool.wait_ge(h2_split, TT * b + t + 1)
                    cols = slice(t * P, (t + 1) * P)
                    nc.gpsimd.tensor_tensor(h2_lo[:, :, cols], x_more[:, t, :].rearrange("p (k c) -> p k c", c=P),
                                            h2_hi[:, :, cols].bitcast(F32), ALU.subtract).then_inc(h2_ready, 1)

            loops(pool, start, step, end)

        def norm_evacuate(eng_is_act, which, b, t):
            for k in range(KT):
                src = tail[:, (t % 2) * N + k * P:(t % 2) * N + (k + 1) * P]
                dst = h1[:, k, t * P:(t + 1) * P] if which == 0 else x_more[:, t, k * P:(k + 1) * P]
                sh = mod[:, 2 * KT * which + k:2 * KT * which + k + 1]
                sc = mod[:, 2 * KT * which + KT + k:2 * KT * which + KT + k + 1]
                if eng_is_act:
                    done = nc.scalar.activation(dst, src, ACT.Identity, bias=sh, scale=sc)
                else:
                    done = nc.vector.tensor_scalar(dst, src, sc, sh, ALU.mult, ALU.add)
            done.then_inc((even_out if eng_is_act else odd_out)[which], 1)

        @block.scalar
        def _(act):
            act.wait_ge(small_loaded, 48)
            nc.scalar.activation(silu[:, :], cond[:, :], ACT.Exp, scale=-1.0).then_inc(silu_exp, 1)

            def norm(which, b):
                act.wait_ge(var_ready[which], b + 1)
                act.wait_ge(consts_ready, 2)
                nc.scalar.activation(std[:, :], mean_var[:, :, 1], ACT.Sqrt, bias=eps_col[:, 0:1]).then_inc(std_ready[which], 1)
                act.wait_ge(mod_ready, b + 1)
                if which == 1:
                    act.wait_ge(out_stored, 16 * b)
                for t in range(0, TT, 2):
                    if which == 1 and t == TT - 2:
                        act.wait_ge(x1_stored, 16 * b + 16)
                    act.wait_ge(norm_t[which], TT * b + t + 1)
                    norm_evacuate(True, which, b, t)

            def start(b):
                act.wait_ge(mask_loaded, 16 * (b + 1))
                act.wait_ge(stacks_primed, 1)
                row = mask_u8[MASK_ROW:MASK_ROW + 1, :].unsqueeze(1).broadcast_to((1, HG, S))
                nc.scalar.activation(k_st[MASK_ROW:MASK_ROW + 1, :, :], row, ACT.Copy, scale=NEG, bias=-NEG).then_inc(mask_rows, 1)
                nc.scalar.activation(q_st[MASK_ROW:MASK_ROW + 1, :, :], row, ACT.Copy).then_inc(mask_rows, 1)
                norm(0, b)

            def step(n, g, m, b):
                if n is not None:
                    act.wait_ge(q_full_ready, HALVES * (n + 1))
                    nc.scalar.activation(q_hi[:, :], qf[:, :], ACT.Copy).then_inc(q_hi_ready, 1)
                    act.wait_ge(k_full_ready, HALVES * (n + 1))
                    nc.scalar.activation(k_hi[:, :], kf[:, :], ACT.Copy).then_inc(k_hi_ready, 1)
                    for half in range(HALVES):
                        cols = slice(half * N, (half + 1) * N)
                        act.wait_ge(qkv_full, 3 * HALVES * n + 2 * HALVES + half + 1)
                        nc.scalar.activation(v_ch[:, cols], pair[2][:, cols], ACT.Identity,
                                             bias=w_qkv[:, QKV_W + 2:QKV_W + 3]).then_inc(v_ch_ready, 1)
                if m is not None:
                    act.wait_ge(proj_full, TT * n if n is not None else TT * G * B)
                    for i in range(JT * HALVES):
                        j = i // HALVES
                        act.wait_ge(fc1_full, JT * HALVES * m + i + 1)
                        if i >= 4:
                            act.wait_ge(u_ready, JT * HALVES * m + i - 3)
                        nc.scalar.activation(u_full[:, i % 4, :], tail[:, (i % 2) * N:(i % 2 + 1) * N], ACT.Gelu_apprx_tanh,
                                             bias=fc1_bias[:, j:j + 1]).then_inc(gelu_ready, 1)
                if n is not None:
                    for t in range(TILES):
                        act.wait_ge(neg_max_ready, TILES * n + t + 1)
                        nc.scalar.activation(pair[t % 3][:, :], pair[t % 3][:, :], ACT.Exp, bias=neg_max[:, t:t + 1],
                                             accum_out=den[:, t:t + 1]).then_inc(den_ready, 1)
                    if m is not None:
                        act.wait_ge(fc2_full, TT * (m + 1))
                    for t in range(TILES):
                        kt, h = t // HG, t % HG
                        act.wait_ge(score_t_full, TILES * n + t + 1)
                        if kt >= 2 and h == 0:
                            act.wait_ge(probs_used, TT * n + kt - 1)
                        nc.scalar.activation(probs[:, (kt % 2) * HG + h, :], pair[t % 3][:, :], ACT.Exp).then_inc(probs_ready, 1)

            def end(b, with_mlp):
                norm(1, b)

            loops(act, start, step, end)

        @block.vector
        def _(dve):
            nc.vector.memset(k_st[STACK:STACK + 3, :, :].bitcast(F32), 1.0).then_inc(stacks_primed, 1)
            dve.wait_ge(silu_exp, 1)
            nc.vector.tensor_scalar(silu[:, :], silu[:, :], 1.0, None, ALU.add).then_inc(silu_step, 1)
            dve.wait_ge(silu_step, 1)
            nc.vector.reciprocal(silu[:, :], silu[:, :]).then_inc(silu_step, 1)
            dve.wait_ge(silu_step, 2)
            nc.vector.tensor_tensor(silu[:, :], silu[:, :], cond[:, :], ALU.mult).then_inc(silu_ready, 1)
            for i, row in ((2, 0), (5, 1)):
                dve.wait_ge(ada_done, i + 1)
                nc.vector.tensor_tensor(gate_rows[:, row * C:(row + 1) * C], pair[row][0:B, 0:N],
                                        gate_bias[:, row * C:(row + 1) * C], ALU.add).then_inc(gates_ready, 1)
            dve.wait_ge(ada_done, 6)
            for b in range(B):
                last = nc.vector.tensor_tensor(mod_all[:, b, :], tail[:, 0:NMOD * B].rearrange("p (f b) -> p b f", b=B)[:, b, :],
                                               ada_bias[:, :], ALU.add)
            last.then_inc(mod_step, 1)
            dve.wait_ge(mod_step, 1)
            for which in range(2):
                sc = mod_all[:, :, (2 * which + 1) * KT:(2 * which + 2) * KT]
                last = nc.vector.tensor_scalar(sc, sc, 1.0, None, ALU.add)
            last.then_inc(mod_step, 1)
            dve.wait_ge(mod_step, 2)

            def normalize(which, b, src, dst):
                for t in range(TT):
                    last = nc.vector.bn_stats(bn6[:, t, :], src[:, t, :])
                last.then_inc(norm_step, 1)
                dve.wait_ge(norm_step, 6 * b + 3 * which + 1)
                nc.vector.memset(shift[:, :], 0.0)
                for t in range(TT):
                    last = nc.vector.bn_aggr(mean_var[:, t, :], bn6[:, t, :])
                last.then_inc(var_ready[which], 1)
                dve.wait_ge(std_ready[which], b + 1)
                nc.vector.reciprocal(rstd[:, :], std[:, :]).then_inc(norm_step, 1)
                dve.wait_ge(norm_step, 6 * b + 3 * which + 2)
                nc.vector.scalar_tensor_tensor(out=shift[:, :], in0=mean_var[:, :, 0], scalar=-1.0, in1=rstd[:, :],
                                               op0=ALU.mult, op1=ALU.mult).then_inc(norm_step, 1)
                dve.wait_ge(norm_step, 6 * b + 3 * which + 3)
                for t in range(TT):
                    nc.vector.tensor_scalar(dst[:, t, :], src[:, t, :], rstd[:, t:t + 1], shift[:, t:t + 1],
                                            ALU.mult, ALU.add).then_inc(norm_ready[which], 1)
                if which == 1:
                    dve.wait_ge(out_stored, 16 * b)
                for t in range(TT):
                    if t % 2:
                        dve.wait_ge(norm_t[which], TT * b + t + 1)
                        norm_evacuate(False, which, b, t)
                    if which == 1:
                        if t % 2:
                            dve.wait_ge(odd_out[1], TT // 2 * b + t // 2 + 1)
                        else:
                            dve.wait_ge(even_out[1], TT // 2 * b + t // 2 + 1)
                        nc.vector.tensor_copy(h2_hi[:, :, t * P:(t + 1) * P],
                                              x_more[:, t, :].rearrange("p (k c) -> p k c", c=P)).then_inc(h2_split, 1)

            def start(b):
                dve.wait_ge(even_out[1], TT // 2 * b)
                nc.vector.tensor_copy(mod[:, :], mod_all[:, bass.ds(b, 1), :].rearrange("p o f -> p (o f)")).then_inc(mod_ready, 1)
                dve.wait_ge(mask_loaded, 16 * (b + 1))
                nc.vector.tensor_scalar(q_mask[:, :], mask_u8[:, :], SCALE, None, ALU.mult).then_inc(mask_ready, 1)
                dve.wait_ge(mod_ready, b + 1)
                dve.wait_ge(x_loaded, 16 * (b + 1))
                normalize(0, b, x_tiles, x_tiles)

            def split_high(part, m):
                dve.wait_ge(raw_loaded, 32 * m + 16 * (part + 1))
                for c in range(FC2_W // N):
                    cols = slice(c * N, (c + 1) * N)
                    done = nc.vector.tensor_copy(w_hi[:, cols], w_raw[:, cols])
                if part == 0:
                    done = nc.vector.tensor_copy(fc1_bias[:, :], w_raw[:, FC1_W:FC1_W + JT])
                done.then_inc(w_hi_ready, 1)

            def fc2_add(m, tt):
                dve.wait_ge(fc2_full, TT * m + tt + 1)
                nc.vector.tensor_tensor(mlp_acc[:, tt, :], tail[:, (tt % 2) * N:(tt % 2 + 1) * N], mlp_acc[:, tt, :],
                                        ALU.add).then_inc(fc2_added, 1)

            def step(n, g, m, b):
                if m is not None:
                    split_high(0, m)
                if n is not None:
                    for i, (dst, msk, ready) in enumerate(((qf, q_mask, q_full_ready), (kf, mask_u8, k_full_ready))):
                        for half in range(HALVES):
                            cols = slice(half * N, (half + 1) * N)
                            dve.wait_ge(qkv_full, 3 * HALVES * n + HALVES * i + half + 1)
                            nc.vector.scalar_tensor_tensor(out=dst[:, cols], in0=pair[i][:, cols],
                                                           scalar=w_qkv[:, QKV_W + i:QKV_W + i + 1], in1=msk[:, cols],
                                                           op0=ALU.add, op1=ALU.mult).then_inc(ready, 1)
                    dve.wait_ge(v_t, n + 1)
                    nc.vector.tensor_copy(v_tok[:, :, :].rearrange("p t c -> p (t c)"), pair[0][:, :]).then_inc(v_ready, 1)
                if m is not None:
                    if n is not None:
                        dve.wait_ge(stack_loaded, 16 * 6 * HG * (n + 1))
                    for i in range(JT * HALVES):
                        j, half = i // HALVES, i % HALVES
                        dve.wait_ge(gelu_ready, JT * HALVES * m + i + 1)
                        nc.vector.tensor_copy(u_hi[:, j, half * N:(half + 1) * N], u_full[:, i % 4, :]).then_inc(u_hi_ready, 1)
                    dve.wait_ge(mlp_acc_loaded, 16 * b)
                    dve.wait_ge(fc1_full, JT * HALVES * (m + 1))
                    split_high(1, m)
                if n is not None:
                    for t in range(TILES):
                        if m is not None and t in fc2_at:
                            fc2_add(m, fc2_at[t])
                        dve.wait_ge(score_full, TILES * n + t + 1)
                        nc.vector.tensor_reduce(neg_max[:, t:t + 1], pair[t % 3][:, :], AX_X, ALU.max,
                                                negate=True).then_inc(neg_max_ready, 1)
                    dve.wait_ge(neg_max_ready, TILES * (n + 1))
                    nc.vector.tensor_copy(stat[:, 0:TILES].bitcast(F32R), neg_max[:, :]).then_inc(stat_step, 1)
                    dve.wait_ge(stat_step, n + 1)
                    nc.vector.tensor_tensor(stat[:, TILES:2 * TILES], neg_max[:, :], stat[:, 0:TILES], ALU.subtract)
                    dve.wait_ge(den_ready, TILES * (n + 1))
                    nc.vector.reciprocal(stat[:, 2 * TILES:3 * TILES], den[:, :]).then_inc(stat_ready, 1)
                if m is not None:
                    if n is None:
                        for tt in range(TT - 1):
                            fc2_add(m, tt)
                    fc2_add(m, TT - 1)
                if n is not None:
                    dve.wait_ge(stat_turned, n + 1)
                    nc.vector.tensor_copy(stat_t[:, :], pair[2][0:3 * TILES, 0:P]).then_inc(stat_t_ready, 1)
                    dve.wait_ge(den_spread, n + 1)
                    nc.vector.tensor_copy(den_bc[:, :], pair[2][:, :]).then_inc(den_bc_ready, 1)
                    dve.wait_ge(den_bc_ready, n + 1)
                    dve.wait_ge(probs_used, TT * (n + 1))
                    for half in range(HALVES):
                        cols = slice(half * N, (half + 1) * N)
                        nc.vector.tensor_tensor(attn_ch[:, cols], tail[:, cols], den_bc[:, cols], ALU.mult).then_inc(attn_ready, 1)
                    dve.wait_ge(acc_loaded, 16 * (b + 1))
                    for tt in range(TT):
                        dve.wait_ge(proj_full, TT * n + tt + 1)
                        nc.vector.tensor_tensor(attn_acc[:, tt, :], pair[tt // 2 % 2][:, (tt % 2) * N:(tt % 2 + 1) * N],
                                                attn_acc[:, tt, :], ALU.add).then_inc(proj_added, 1)

            def multiply_add(acc, gate, res, wait_value):
                for t in range(TT):
                    last = nc.vector.tensor_tensor(acc[:, t, :], acc[:, t, :], gate[:, :], ALU.mult)
                last.then_inc(gated, 1)
                dve.wait_ge(gated, wait_value)
                for t in range(TT):
                    last = nc.vector.tensor_tensor(res[:, t, :], res[:, t, :], acc[:, t, :], ALU.add)
                return last

            def end(b, with_mlp):
                if with_mlp:
                    dve.wait_ge(x1_again, 32 * b)
                    dve.wait_ge(fc2_added, TT * G * b)
                    multiply_add(mlp_acc, gate2, x_more, 2 * b).then_inc(final_ready, 1)
                dve.wait_ge(x_again, 32 * (b + 1))
                dve.wait_ge(proj_added, TT * G * (b + 1))
                multiply_add(attn_acc, gate1, x_tiles, 2 * b + 1).then_inc(x1_ready, 1)
                dve.wait_ge(x1_ready, b + 1)
                normalize(1, b, x_tiles, attn_acc)

            loops(dve, start, step, end)
            dve.wait_ge(x1_again, 32 * B)
            dve.wait_ge(fc2_added, TT * G * B)
            multiply_add(mlp_acc, gate2, x_more, 2 * B).then_inc(final_ready, 1)

        @block.tensor
        def _(pe):
            pe.wait_ge(silu_ready, 1)
            sl = silu[:, :].rearrange("p (k b) -> p k b", b=B)
            vec = 0
            for i in range(6):
                pe.wait_ge(ada_loaded[i], 16)
                if i in (2, 5):
                    for k in range(KT):
                        last = nc.tensor.matmul(pair[i // 3][0:B, 0:N], sl[:, k, :], ada_w[:, i % 4, k, :], start=k == 0, stop=k == KT - 1)
                else:
                    for f in range(KT):
                        col = (vec * KT + f) * B
                        for k in range(KT):
                            last = nc.tensor.matmul(tail[:, col:col + B], ada_w[:, i % 4, k, f * P:(f + 1) * P], sl[:, k, :],
                                                    start=k == 0, stop=k == KT - 1)
                    vec += 1
                last.then_inc(ada_done, 1)
            pe.wait_ge(consts_ready, 2)
            pe.wait_ge(mod_step, 1)
            pe.wait_ge(gates_ready, 2)

            def transposes(which, b, src):
                for t in range(TT):
                    pe.wait_ge(norm_ready[which], TT * b + t + 1)
                    if t >= 2:
                        if t % 2:
                            pe.wait_ge(odd_out[which], TT // 2 * b + t // 2)
                        else:
                            pe.wait_ge(even_out[which], TT // 2 * b + t // 2)
                    for k in range(KT):
                        o = (t % 2) * N + k * P
                        last = nc.tensor.transpose(tail[:, o:o + P], src[:, t, k * P:(k + 1) * P], ident[:, :])
                    last.then_inc(norm_t[which], 1)

            def start(b):
                pe.wait_ge(even_out[1], TT // 2 * b)
                pe.wait_ge(odd_out[1], TT // 2 * b)
                transposes(0, b, x_tiles)

            def fc1(m, i):
                j, half = i // HALVES, i % HALVES
                if i >= 2:
                    pe.wait_ge(gelu_ready, JT * HALVES * m + i - 1)
                dst = tail[:, (i % 2) * N:(i % 2 + 1) * N]
                terms = [(w, h) for w, h in ((w_lo, h2_hi), (w_hi, h2_lo), (w_hi, h2_hi))]
                for a, (w, h) in enumerate(terms):
                    for k in range(KT):
                        last = nc.tensor.matmul(dst, w[:, (k * JT + j) * P:(k * JT + j + 1) * P], h[:, k, half * N:(half + 1) * N],
                                                start=a == 0 and k == 0, stop=a == 2 and k == KT - 1)
                last.then_inc(fc1_full, 1)

            def fc2(m, tt):
                if tt >= 2:
                    pe.wait_ge(fc2_added, TT * m + tt - 1)
                else:
                    pe.wait_ge(gelu_ready, JT * HALVES * (m + 1))
                if tt == 0:
                    pe.wait_ge(u_ready, JT * HALVES * (m + 1))
                    pe.wait_ge(w_ready, 2 * m + 2)
                dst = tail[:, (tt % 2) * N:(tt % 2 + 1) * N]
                for a, (u, w) in enumerate(((u_lo, w_hi), (u_hi, w_lo), (u_hi, w_hi))):
                    for j in range(JT):
                        last = nc.tensor.matmul(dst, u[:, j, tt * P:(tt + 1) * P], w[:, j * C:(j + 1) * C],
                                                start=a == 0 and j == 0, stop=a == 2 and j == JT - 1)
                last.then_inc(fc2_full, 1)

            def step(n, g, m, b):
                if n is not None:
                    pe.wait_ge(wqkv_loaded, 16 * (n + 1))
                    pe.wait_ge(even_out[0], TT // 2 * (b + 1))
                    pe.wait_ge(odd_out[0], TT // 2 * (b + 1))
                    for i in range(3):
                        for half in range(HALVES):
                            for k in range(KT):
                                last = nc.tensor.matmul(pair[i][:, half * N:(half + 1) * N], w_qkv[:, (i * KT + k) * P:(i * KT + k + 1) * P],
                                                        h1[:, k, half * N:(half + 1) * N], start=k == 0, stop=k == KT - 1)
                            last.then_inc(qkv_full, 1)
                if m is not None:
                    pe.wait_ge(w_ready, 2 * m + 1)
                    pe.wait_ge(h2_ready, TT * b)
                    fc1(m, 0)
                if n is not None:
                    pe.wait_ge(v_ch_ready, HALVES * (n + 1))
                    pe.wait_ge(q_full_ready, HALVES * (n + 1))
                    for t in range(TT):
                        last = nc.tensor.transpose(pair[0][:, t * P:(t + 1) * P], v_ch[:, t * P:(t + 1) * P], ident[:, :])
                    last.then_inc(v_t, 1)
                if m is not None:
                    for i in range(1, JT * HALVES):
                        fc1(m, i)
                if n is not None:
                    pe.wait_ge(stack_loaded, 16 * 6 * HG * (n + 1))
                    pe.wait_ge(mask_rows, 2 * (b + 1))
                    pe.wait_ge(v_ready, n + 1)
                    pe.wait_ge(k_full_ready, HALVES * (n + 1))
                    for t in range(TILES):
                        h, qt = t // TT, t % TT
                        if m is not None and t in fc2_at:
                            fc2(m, fc2_at[t])
                        if t >= 3:
                            pe.wait_ge(den_ready, TILES * n + t - 2)
                        for half in range(HALVES):
                            last = nc.tensor.matmul(pair[t % 3][:, half * N:(half + 1) * N], q_st[0:MAX_ROW, h, qt * P:(qt + 1) * P],
                                                    k_st[0:MAX_ROW, h, half * N:(half + 1) * N], start=True, stop=True)
                        last.then_inc(score_full, 1)
                if m is not None:
                    if n is None:
                        for tt in range(TT - 1):
                            fc2(m, tt)
                    fc2(m, TT - 1)
                if n is not None:
                    pe.wait_ge(stat_ready, n + 1)
                    nc.tensor.transpose(pair[2][0:3 * TILES, 0:P], stat[:, :], ident[:, :]).then_inc(stat_turned, 1)
                    pe.wait_ge(rows_loaded, 16 * (2 + HG) * (n + 1))
                    pe.wait_ge(stat_t_ready, n + 1)

                    def weigh(kt):
                        pe.wait_ge(probs_ready, TILES * n + HG * (kt + 1))
                        for half in range(HALVES):
                            for h in range(HG):
                                last = nc.tensor.matmul(tail[h * HD:(h + 1) * HD, half * N:(half + 1) * N],
                                                        v_tok[:, kt, h * HD:(h + 1) * HD],
                                                        probs[:, (kt % 2) * HG + h, half * N:(half + 1) * N],
                                                        start=kt == 0, stop=kt == TT - 1)
                        last.then_inc(probs_used, 1)

                    if m is not None:
                        pe.wait_ge(fc2_added, TT * (m + 1))
                    for kt in range(TT):
                        for h in range(HG):
                            t = kt * HG + h
                            if t >= 3:
                                pe.wait_ge(probs_ready, TILES * n + t - 2)
                            for half in range(HALVES):
                                last = nc.tensor.matmul(pair[t % 3][:, half * N:(half + 1) * N], k_st[0:MAX_ROW + 2, h, kt * P:(kt + 1) * P],
                                                        q_st[0:MAX_ROW + 2, h, half * N:(half + 1) * N], start=True, stop=True)
                            last.then_inc(score_t_full, 1)
                        if kt:
                            weigh(kt - 1)
                    pe.wait_ge(probs_ready, TILES * n + TILES - 2)
                    for half in range(HALVES):
                        last = nc.tensor.matmul(pair[2][:, half * N:(half + 1) * N], head_sel[:, :], den_row[:, half * N:(half + 1) * N],
                                                start=True, stop=True)
                    last.then_inc(den_spread, 1)
                    weigh(TT - 1)
                    pe.wait_ge(wproj_loaded, 16 * (n + 1))
                    for tt in range(TT):
                        pe.wait_ge(attn_ready, HALVES * n + tt // (TT // HALVES) + 1)
                        if tt >= 4:
                            pe.wait_ge(proj_added, TT * n + tt - 3)
                        nc.tensor.matmul(pair[tt // 2 % 2][:, (tt % 2) * N:(tt % 2 + 1) * N], attn_ch[:, tt * P:(tt + 1) * P],
                                         w_proj[:, :], start=True, stop=True).then_inc(proj_full, 1)
                    pe.wait_ge(proj_added, TT * (n + 1))

            def end(b, with_mlp):
                transposes(1, b, attn_acc)

            loops(pe, start, step, end)


def kernel(x, cond_1024, mask_BxS_bk1, L0_cond_qkv_w, L0_cond_qkv_b, L0_cond_proj_w, L0_cond_proj_b,
           L0_cond_fc1_w, L0_cond_fc1_b, L0_cond_fc2_w, L0_cond_fc2_b, L0_cond_ada_w, L0_cond_ada_b):
    import numpy as np
    import concourse.bacc as bacc
    from concourse.bass_utils import run_bass_kernel_spmd

    def rows(a):
        return np.ascontiguousarray(a)

    def wrapped(a):
        return np.concatenate([a, a[:1]], axis=0)

    qkv = np.asarray(L0_cond_qkv_w).reshape(3, G, P, KT, P).transpose(1, 4, 0, 3, 2).reshape(G, P, QKV_W)
    qkv_b = np.asarray(L0_cond_qkv_b).reshape(3, G, P).transpose(1, 2, 0)
    fc1 = np.asarray(L0_cond_fc1_w).reshape(G, JT * P, KT, P).transpose(0, 3, 2, 1).reshape(G, P, FC1_W)
    fc1_b = np.asarray(L0_cond_fc1_b).reshape(G, JT, P).transpose(0, 2, 1)
    fc2 = np.asarray(L0_cond_fc2_w).reshape(C, G, JT, P).transpose(1, 3, 2, 0).reshape(G, P, FC2_W)
    ada = np.asarray(L0_cond_ada_w).reshape(6, C, KT, P).transpose(0, 3, 2, 1)
    ada_b = np.asarray(L0_cond_ada_b).reshape(6, KT, P)
    arrays = {
        "x": rows(x),
        "cond_t": rows(np.asarray(cond_1024).reshape(B, KT, P).transpose(2, 1, 0).reshape(P, KT * B)),
        "mask": rows(mask_BxS_bk1),
        "wqkv": rows(wrapped(np.concatenate([qkv, qkv_b], axis=2))),
        "wproj": rows(wrapped(np.asarray(L0_cond_proj_w).T.reshape(G, P, C))),
        "wfc1": rows(wrapped(np.concatenate([fc1, fc1_b], axis=2))),
        "wfc2": rows(fc2),
        "proj_b": rows(np.asarray(L0_cond_proj_b).reshape(1, 1, C)),
        "fc2_b": rows(np.asarray(L0_cond_fc2_b).reshape(1, 1, C)),
        "ada_wt": rows(ada),
        "ada_bt": rows(ada_b[[0, 1, 3, 4]].transpose(2, 0, 1).reshape(P, NMOD)),
        "ada_bg": rows(ada_b[[2, 5]].reshape(1, 2 * C)),
    }
    nc = bacc.Bacc("TRN2", target_bir_lowering=False, num_devices=1)
    args = [nc.dram_tensor(f"in_{n}", a.shape, mybir.dt.from_np(a.dtype), kind="ExternalInput").ap() for n, a in arrays.items()]
    out = nc.dram_tensor("out_x", (B, S, C), F32, kind="ExternalOutput").ap()
    block_kernel(nc, *args, out)
    r = run_bass_kernel_spmd(nc, [{f"in_{n}": a for n, a in arrays.items()}], core_ids=[0])
    return r.results[0]["out_x"]
```

```python
from contextlib import ExitStack

import concourse.bass as bass
from concourse import mybir

F32 = mybir.dt.float32
F32R = mybir.dt.float32r
U8 = mybir.dt.uint8
ALU = mybir.AluOpType
ACT = mybir.ActivationFunctionType
AX_X = mybir.AxisListType.X

B, S, C = 4, 1024, 512
HEADS, HD, HIDDEN = 16, 32, 2048
EPS = 1e-6
P = 128
KT = C // P
TT = S // P
G = C // P
HG = HEADS // G
JT = HIDDEN // G // P
N = 512
HALVES = S // N
TILES = HG * TT
STACK = 3 * HD
MASK_ROW = STACK
MAX_ROW = STACK + 1
SCALE = HD ** -0.5
NEG = 1.0e9
QKV_W = 3 * KT * P
FC1_W = KT * JT * P
FC2_W = JT * C
NMOD = 4 * KT
FC2_FIRST = 7
FC2_INSIDE = 5
PROJ_PAIR = (0, 1, 2, 1)
SPREAD_AT = 6


def known(index, value):
    return isinstance(index, int) and index == value


def fc2_schedule():
    pieces, adds = {}, {}
    for i in range(3 * FC2_INSIDE):
        t = FC2_FIRST + i * (TILES - FC2_FIRST) // (3 * FC2_INSIDE)
        pieces.setdefault(t, []).append((i // 3, i % 3))
        if i % 3 == 2:
            adds[min(t + 1, TILES - 1)] = i // 3
    return pieces, adds


def block_kernel(nc, x, cond_t, mask, wqkv, wproj, wfc1, wfc2, proj_b, fc2_b, ada_wt, ada_bt, ada_bg, out):
    x1_dram = nc.dram_tensor("x1_dram", (B, S, C), F32, kind="Internal").ap()
    gate_dram = nc.dram_tensor("gate_dram", (B, 2 * C), F32, kind="Internal").ap()
    fc2_pieces, fc2_adds = fc2_schedule()

    with ExitStack() as ctx:
        def sb(name, shape, dt=F32):
            return ctx.enter_context(nc.sbuf_tensor(name, shape, dt))

        def sem(name):
            return ctx.enter_context(nc.semaphore(name))

        w_qkv = sb("w_qkv", [P, QKV_W + 3])
        w_proj = sb("w_proj", [P, C])
        w_raw = sb("w_raw", [P, FC1_W + JT])
        w_hi = sb("w_hi", [P, FC1_W], F32R)
        w_lo = sb("w_lo", [P, FC1_W], F32R)
        fc1_bias = sb("fc1_bias", [P, JT])
        attn_acc = sb("attn_acc", [P, TT, C])
        x_next = sb("x_next", [P, TT, C])
        mlp_acc = sb("mlp_acc", [P, TT, C])
        h1 = sb("h1", [P, KT, S])
        q_st = sb("q_st", [P, HG, S], F32R)
        k_st = sb("k_st", [P, HG, S], F32R)
        v_tok = sb("v_tok", [P, TT, P])
        q_mask = sb("q_mask", [P, S])
        mask_u8 = sb("mask_u8", [P, S], U8)
        gate1 = sb("gate1", [P, C])
        gate2 = sb("gate2", [P, C])
        den_row = sb("den_row", [HG, S])
        ident = sb("ident", [P, P])
        head_sel = sb("head_sel", [HG, P])
        neg_max = sb("neg_max", [P, TILES])
        den = sb("den", [P, TILES])
        stat = sb("stat", [P, 3 * TILES])
        stat_t = sb("stat_t", [3 * TILES, P])
        mod_all = sb("mod_all", [P, B, NMOD])
        mod = sb("mod", [P, NMOD])
        eps_col = sb("eps_col", [P, 1])
        bn6 = sb("bn6", [P, TT, 6])
        mean_var = sb("mean_var", [P, TT, 2])
        std = sb("std", [P, TT])
        rstd = sb("rstd", [P, TT])
        shift = sb("shift", [P, TT])
        ada_bias = sb("ada_bias", [P, NMOD])
        cond = sb("cond", [P, KT * B])
        silu = sb("silu", [P, KT * B])

        def in_turn(*layouts):
            made = []
            for layout in layouts:
                with ExitStack() as turn:
                    made.append([turn.enter_context(nc.sbuf_tensor(n, s, d)) for n, s, d in layout])
            return made

        (h2_hi, h2_lo), (ada_w,) = in_turn(
            [("h2_hi", [P, KT, S], F32R), ("h2_lo", [P, KT, S], F32R)],
            [("ada_w", [P, 4, KT, C], F32)],
        )
        ctx.enter_context(nc.sbuf_tensor("h2_region", [P, 2 * KT * S], F32))
        big = in_turn(
            [("u_hi", [P, JT, S], F32R), ("u_lo", [P, JT, S], F32R)],
            [("probs", [P, 2 * HG, S], F32)],
            [("qf", [P, S], F32), ("kf", [P, S], F32), ("q_hi", [P, S], F32R), ("q_lo", [P, S], F32R),
             ("k_hi", [P, S], F32R), ("k_lo", [P, S], F32R), ("v_ch", [P, S], F32)],
        )
        (u_hi, u_lo), (probs,), (qf, kf, q_hi, q_lo, k_hi, k_lo, v_ch) = big
        ctx.enter_context(nc.sbuf_tensor("big_region", [P, 2 * HG * S], F32))
        (gate_bias, gate_rows), (u_full,), (attn_ch, den_bc) = in_turn(
            [("gate_bias", [B, 2 * C], F32), ("gate_rows", [B, 2 * C], F32)],
            [("u_full", [P, 4, N], F32)],
            [("attn_ch", [P, S], F32), ("den_bc", [P, S], F32)],
        )
        ctx.enter_context(nc.sbuf_tensor("small_region", [P, 2 * S], F32))

        pair = [ctx.enter_context(nc.psum_tensor(f"pair{i}", [P, S], F32)) for i in range(3)]
        tail = ctx.enter_context(nc.psum_tensor("tail", [P, S], F32))

        consts_ready = sem("consts_ready")
        ident_zero = sem("ident_zero")
        stacks_primed = sem("stacks_primed")
        small_loaded = sem("small_loaded")
        ada_loaded = [sem(f"ada_loaded{i}") for i in range(6)]
        silu_step = sem("silu_step")
        silu_exp = sem("silu_exp")
        silu_ready = sem("silu_ready")
        ada_done = sem("ada_done")
        gates_ready = sem("gates_ready")
        mod_step = sem("mod_step")
        gates_stored = sem("gates_stored")
        x_loaded = sem("x_loaded")
        mask_loaded = sem("mask_loaded")
        mask_ready = sem("mask_ready")
        mask_rows = sem("mask_rows")
        mod_ready = [sem("mod1_ready"), sem("mod2_ready")]
        acc_loaded = sem("acc_loaded")
        var_ready = [sem("var1_ready"), sem("var2_ready")]
        std_ready = [sem("std1_ready"), sem("std2_ready")]
        norm_ready = [sem("norm1_ready"), sem("norm2_ready")]
        norm_t = [sem("norm1_t"), sem("norm2_t")]
        even_out = [sem("even1_out"), sem("even2_out")]
        odd_out = [sem("odd1_out"), sem("odd2_out")]
        norm_step = [sem("norm1_step"), sem("norm2_step")]
        x1_gated = sem("x1_gated")
        mlp_gated = sem("mlp_gated")
        h2_split = sem("h2_split")
        h2_ready = sem("h2_ready")
        gates_loaded = sem("gates_loaded")
        x_again = sem("x_again")
        x1_ready = sem("x1_ready")
        x1_stored = sem("x1_stored")
        x1_again = sem("x1_again")
        final_ready = sem("final_ready")
        out_stored = sem("out_stored")
        mlp_acc_loaded = sem("mlp_acc_loaded")
        wqkv_loaded = sem("wqkv_loaded")
        wproj_loaded = sem("wproj_loaded")
        qkv_full = sem("qkv_full")
        q_full_ready = sem("q_full_ready")
        k_full_ready = sem("k_full_ready")
        q_hi_ready = sem("q_hi_ready")
        k_hi_ready = sem("k_hi_ready")
        q_lo_ready = sem("q_lo_ready")
        k_lo_ready = sem("k_lo_ready")
        v_ch_ready = sem("v_ch_ready")
        v_t = sem("v_t")
        v_ready = sem("v_ready")
        stack_loaded = sem("stack_loaded")
        score_full = sem("score_full")
        neg_max_ready = sem("neg_max_ready")
        exp_done = sem("exp_done")
        stat_step = sem("stat_step")
        stat_ready = sem("stat_ready")
        stat_turned = sem("stat_turned")
        stat_t_ready = sem("stat_t_ready")
        rows_loaded = sem("rows_loaded")
        den_loaded = sem("den_loaded")
        score_t_full = sem("score_t_full")
        probs_used = sem("probs_used")
        den_spread = sem("den_spread")
        den_bc_ready = sem("den_bc_ready")
        attn_ready = sem("attn_ready")
        proj_full = sem("proj_full")
        proj_added = sem("proj_added")
        raw_loaded = sem("raw_loaded")
        w_hi_ready = sem("w_hi_ready")
        w_ready = sem("w_ready")
        fc1_full = sem("fc1_full")
        gelu_ready = sem("gelu_ready")
        u_hi_ready = sem("u_hi_ready")
        u_ready = sem("u_ready")
        fc2_full = sem("fc2_full")
        fc2_added = sem("fc2_added")

        block = ctx.enter_context(nc.Block())

        def row_block(dram, b):
            return dram[bass.ds(b, 1)].rearrange("o (t p) c -> p (o t) c", p=P)

        def ring(t):
            return t if t < SPREAD_AT else t + 1

        def at(dram, i):
            return dram[bass.ds(i, 1)].rearrange("o p c -> (o p) c")

        def loops(eng, step):
            step(0, 0, None, 0)
            with eng.Fori(1, G - 1) as g:
                step(g, g, None, 0)
            step(G - 1, G - 1, None, 0, ln1=1)

            def batch(b, ln1):
                step(b * G, 0, b * G - G, b, ln2=b - 1)
                with eng.Fori(1, G - 1) as g:
                    step(b * G + g, g, b * G + g - G, b)
                step(b * G + G - 1, G - 1, b * G - 1, b, ln1=ln1, fin=b - 1)

            with eng.Fori(1, B - 1) as b:
                batch(b, b + 1)
            batch(B - 1, None)

        @block.sync
        def _(sp):
            sp.dma_start(cond[:, :], cond_t).then_inc(small_loaded, 16)
            sp.dma_start(ada_bias[:, :], ada_bt).then_inc(small_loaded, 16)
            sp.dma_start(gate_bias[:, :], ada_bg.broadcast_to((B, 2 * C))).then_inc(small_loaded, 16)
            sp.dma_start(x_next[:, :, :], row_block(x, 0)).then_inc(x_loaded, 16)
            for i in range(2):
                sp.dma_start(ada_w[:, i], ada_wt[i]).then_inc(ada_loaded[i], 16)
            sp.dma_start(mask_u8[:, :], mask[0:1].broadcast_to((P, S))).then_inc(mask_loaded, 16)
            sp.dma_start(w_qkv[:, :], at(wqkv, 0)).then_inc(wqkv_loaded, 16)
            for i in range(2, 4):
                sp.dma_start(ada_w[:, i], ada_wt[i]).then_inc(ada_loaded[i], 16)
            sp.wait_ge(ada_done, 2)
            for i in range(4, 6):
                sp.dma_start(ada_w[:, i - 4], ada_wt[i]).then_inc(ada_loaded[i], 16)
            sp.dma_start(w_proj[:, :], at(wproj, 0)).then_inc(wproj_loaded, 16)
            sp.dma_start(attn_acc[:, :, :], proj_b.broadcast_to((P, TT, C))).then_inc(acc_loaded, 16)
            sp.dma_start(w_raw[:, :], at(wfc1, 0)).then_inc(raw_loaded, 16)
            sp.dma_start(mlp_acc[:, :, :], fc2_b.broadcast_to((P, TT, C))).then_inc(mlp_acc_loaded, 16)

            def stack(n, hi, lo, hi_ready, lo_ready, st, order):
                sp.wait_ge(hi_ready, n + 1)
                for part in sorted(range(3), key=lambda i: order[i]):
                    if order[part] == "l":
                        sp.wait_ge(lo_ready, n + 1)
                    src = hi if order[part] == "h" else lo
                    for h in range(HG):
                        sp.dma_start(st[part * HD:(part + 1) * HD, h, :].bitcast(F32),
                                     src[h * HD:(h + 1) * HD, :].bitcast(F32)).then_inc(stack_loaded, 16)

            def load_fc2(m, g):
                sp.wait_ge(w_ready, 2 * m + 1)
                sp.dma_start(w_raw[:, 0:FC2_W], at(wfc2, g)).then_inc(raw_loaded, 16)

            def load_next_fc1(m, g):
                sp.wait_ge(w_ready, 2 * m + 2)
                sp.dma_start(w_raw[:, :], at(wfc1, g + 1 if not known(g, G - 1) else 0)).then_inc(raw_loaded, 16)

            def step(n, g, m, b, ln1=None, ln2=None, fin=None):
                last_batch = known(b, B - 1)
                if m is not None:
                    load_fc2(m, g)
                stack(n, q_hi, q_lo, q_hi_ready, q_lo_ready, q_st, "hhl")
                if ln2 is not None:
                    sp.wait_ge(x1_ready, b)
                    sp.dma_start(row_block(x1_dram, ln2), x_next[:, :, :]).then_inc(x1_stored, 16)
                stack(n, k_hi, k_lo, k_hi_ready, k_lo_ready, k_st, "hlh")
                if ln1 is not None:
                    sp.dma_start(mask_u8[:, :], mask[bass.ds(ln1, 1)].broadcast_to((P, S))).then_inc(mask_loaded, 16)
                sp.wait_ge(v_ch_ready, HALVES * (n + 1))
                sp.dma_start(w_qkv[:, :], at(wqkv, g + 1)).then_inc(wqkv_loaded, 16)
                if ln2 is not None:
                    sp.wait_ge(norm_t[1], TT * b)
                    sp.dma_start(attn_acc[:, :, :], proj_b.broadcast_to((P, TT, C))).then_inc(acc_loaded, 16)
                if ln1 is not None:
                    sp.wait_ge(norm_t[0], TT * ln1 + TT)
                if fin is not None:
                    sp.dma_start(x_next[:, :, :], row_block(x1_dram, fin)).then_inc(x1_again, 16)
                    sp.dma_start(gate2[:, :], gate_dram[bass.ds(fin, 1), C:2 * C].broadcast_to((P, C))).then_inc(x1_again, 16)
                if m is not None:
                    load_next_fc1(m, g)
                if known(n, 0):
                    sp.wait_ge(gates_ready, 2)
                    sp.dma_start(gate_dram, gate_rows[:, :]).then_inc(gates_stored, 16)
                    sp.wait_ge(gates_stored, 16)
                    sp.wait_ge(norm_t[0], TT)
                    sp.dma_start(x_next[:, :, :], row_block(x, 1)).then_inc(x_loaded, 16)
                sp.wait_ge(stat_t_ready, n + 1)
                sp.dma_start(q_st[MAX_ROW:MAX_ROW + 2, :, :].bitcast(F32).rearrange("r h (t j) -> r (h t) j", j=P),
                             stat_t[0:2 * TILES, :]).then_inc(rows_loaded, 16)
                sp.dma_start(den_row[:, :].rearrange("h (t j) -> h t j", j=P),
                             stat_t[2 * TILES:3 * TILES, :]).then_inc(den_loaded, 16)
                if ln2 is not None:
                    sp.wait_ge(x1_stored, 16 * b)
                    if not last_batch:
                        sp.dma_start(x_next[:, :, :], row_block(x, b + 1)).then_inc(x_loaded, 16)
                if fin is not None:
                    sp.wait_ge(final_ready, b)
                    sp.dma_start(row_block(out, fin), x_next[:, :, :]).then_inc(out_stored, 16)
                    sp.dma_start(mlp_acc[:, :, :], fc2_b.broadcast_to((P, TT, C))).then_inc(mlp_acc_loaded, 16)
                    sp.wait_ge(out_stored, 16 * b)
                if known(g, G - 1):
                    sp.dma_start(x_next[:, :, :], row_block(x, b)).then_inc(x_again, 16)
                    sp.dma_start(gate1[:, :], gate_dram[bass.ds(b, 1), 0:C].broadcast_to((P, C))).then_inc(x_again, 16)
                sp.wait_ge(proj_full, TT * (n + 1))
                sp.dma_start(w_proj[:, :], at(wproj, g + 1)).then_inc(wproj_loaded, 16)

            loops(sp, step)
            sp.dma_start(gate2[:, :], gate_dram[B - 1:B, C:2 * C].broadcast_to((P, C))).then_inc(x1_again, 16)
            with sp.Fori(0, G) as g:
                load_fc2(g + (B - 1) * G, g)
                sp.wait_ge(w_ready, 2 * g + 2 * (B - 1) * G + 2)
                sp.dma_start(w_raw[:, :], at(wfc1, g + 1)).then_inc(raw_loaded, 16)
            sp.wait_ge(final_ready, B)
            sp.dma_start(row_block(out, B - 1), x_next[:, :, :]).then_inc(out_stored, 16)
            sp.wait_ge(wqkv_loaded, 16 * (B * G + 1))
            sp.wait_ge(wproj_loaded, 16 * (B * G + 1))
            sp.wait_ge(raw_loaded, 16 * (2 * B * G + 1))
            sp.wait_ge(acc_loaded, 16 * B)
            sp.wait_ge(x1_stored, 16 * (B - 1))
            sp.wait_ge(out_stored, 16 * B)

        @block.gpsimd
        def _(pool):
            nc.gpsimd.memset(ident[:, :], 0.0).then_inc(ident_zero, 1)
            nc.gpsimd.memset(head_sel[:, :], 1.0).then_inc(ident_zero, 1)
            nc.gpsimd.memset(eps_col[:, :], EPS).then_inc(ident_zero, 1)
            pool.wait_ge(ident_zero, 3)
            nc.gpsimd.affine_select(out=ident[:, :], in_=ident[:, :], compare_op=ALU.not_equal, fill=1.0,
                                    base=0, pattern=[[-1, P]], channel_multiplier=1).then_inc(consts_ready, 1)
            sel = head_sel[:, :].rearrange("p (h d) -> p h d", d=HD)
            nc.gpsimd.affine_select(out=sel, in_=sel, compare_op=ALU.is_equal, fill=0.0,
                                    base=0, pattern=[[-1, HG], [0, HD]], channel_multiplier=1).then_inc(consts_ready, 1)

            def split_low(part, m):
                pool.wait_ge(w_hi_ready, 2 * m + part + 1)
                for c in range(FC2_W // N):
                    cols = slice(c * N, (c + 1) * N)
                    done = nc.gpsimd.tensor_tensor(w_lo[:, cols], w_raw[:, cols], w_hi[:, cols].bitcast(F32), ALU.subtract)
                done.then_inc(w_ready, 1)

            def h2_low(b):
                for t in range(TT):
                    pool.wait_ge(h2_split, TT * b + t + 1)
                    cols = slice(t * P, (t + 1) * P)
                    nc.gpsimd.tensor_tensor(h2_lo[:, :, cols], u_full[:, t % 4, :].rearrange("p (k c) -> p k c", c=P),
                                            h2_hi[:, :, cols].bitcast(F32), ALU.subtract).then_inc(h2_ready, 1)

            def step(n, g, m, b, ln1=None, ln2=None, fin=None):
                if m is not None:
                    split_low(0, m)
                if n is not None:
                    pool.wait_ge(q_hi_ready, n + 1)
                    nc.gpsimd.tensor_tensor(q_lo[:, :], qf[:, :], q_hi[:, :].bitcast(F32), ALU.subtract).then_inc(q_lo_ready, 1)
                    pool.wait_ge(k_hi_ready, n + 1)
                    nc.gpsimd.tensor_tensor(k_lo[:, :], kf[:, :], k_hi[:, :].bitcast(F32), ALU.subtract).then_inc(k_lo_ready, 1)
                if ln2 is not None:
                    h2_low(ln2)
                if m is not None:
                    for i in range(JT * HALVES):
                        j, half = i // HALVES, i % HALVES
                        cols = slice(half * N, (half + 1) * N)
                        pool.wait_ge(u_hi_ready, JT * HALVES * m + i + 1)
                        nc.gpsimd.tensor_tensor(u_lo[:, j, cols], u_full[:, i % 4, :], u_hi[:, j, cols].bitcast(F32),
                                                ALU.subtract).then_inc(u_ready, 1)
                    split_low(1, m)

            loops(pool, step)
            h2_low(B - 1)
            with pool.Fori(0, G) as g:
                step(None, g, g + (B - 1) * G, B)

        def norm_evacuate(eng_is_act, which, b, t):
            for k in range(KT):
                o = (t // 2 % 2) * N + k * P
                src = pair[1 + t % 2][:, o:o + P]
                dst = h1[:, k, t * P:(t + 1) * P] if which == 0 else u_full[:, t % 4, k * P:(k + 1) * P]
                sh = mod[:, 2 * KT * which + k:2 * KT * which + k + 1]
                sc = mod[:, 2 * KT * which + KT + k:2 * KT * which + KT + k + 1]
                if eng_is_act:
                    done = nc.scalar.activation(dst, src, ACT.Identity, bias=sh, scale=sc)
                else:
                    done = nc.vector.tensor_scalar(dst, src, sc, sh, ALU.mult, ALU.add)
            done.then_inc((even_out if eng_is_act else odd_out)[which], 1)

        @block.scalar
        def _(act):
            act.wait_ge(small_loaded, 48)
            nc.scalar.activation(silu[:, :], cond[:, :], ACT.Exp, scale=-1.0).then_inc(silu_exp, 1)

            def standard_deviation(which, b):
                act.wait_ge(var_ready[which], b + 1)
                nc.scalar.activation(std[:, :], mean_var[:, :, 1], ACT.Sqrt, bias=eps_col[:, 0:1]).then_inc(std_ready[which], 1)

            def evacuate(which, b, t):
                if t == 0:
                    act.wait_ge(mod_ready[which], b + 1)
                if which == 1 and t >= 4:
                    act.wait_ge(h2_ready, TT * b + t - 3)
                act.wait_ge(norm_t[which], TT * b + t + 1)
                norm_evacuate(True, which, b, t)

            def set_mask_rows(b):
                act.wait_ge(mask_loaded, 16 * (b + 1))
                act.wait_ge(stacks_primed, 1)
                row = mask_u8[MASK_ROW:MASK_ROW + 1, :].unsqueeze(1).broadcast_to((1, HG, S))
                nc.scalar.activation(k_st[MASK_ROW:MASK_ROW + 1, :, :], row, ACT.Copy, scale=NEG, bias=-NEG).then_inc(mask_rows, 1)
                nc.scalar.activation(q_st[MASK_ROW:MASK_ROW + 1, :, :], row, ACT.Copy).then_inc(mask_rows, 1)

            act.wait_ge(consts_ready, 2)
            standard_deviation(0, 0)
            set_mask_rows(0)
            for t in range(0, TT, 2):
                evacuate(0, 0, t)

            def step(n, g, m, b, ln1=None, ln2=None, fin=None):
                if ln2 is not None:
                    set_mask_rows(b)
                if n is not None:
                    act.wait_ge(q_full_ready, HALVES * (n + 1))
                    nc.scalar.activation(q_hi[:, :], qf[:, :], ACT.Copy).then_inc(q_hi_ready, 1)
                    act.wait_ge(k_full_ready, HALVES * (n + 1))
                    nc.scalar.activation(k_hi[:, :], kf[:, :], ACT.Copy).then_inc(k_hi_ready, 1)
                    if ln1 is not None:
                        standard_deviation(0, ln1)
                    if ln2 is not None:
                        standard_deviation(1, ln2)
                    for half in range(HALVES):
                        cols = slice(half * N, (half + 1) * N)
                        act.wait_ge(qkv_full, 3 * HALVES * n + 2 * HALVES + half + 1)
                        nc.scalar.activation(v_ch[:, cols], pair[2][:, cols], ACT.Identity,
                                             bias=w_qkv[:, QKV_W + 2:QKV_W + 3]).then_inc(v_ch_ready, 1)
                if ln2 is not None:
                    for t in range(0, TT, 2):
                        evacuate(1, ln2, t)
                    act.wait_ge(h2_ready, TT * b)
                if ln1 is not None and m is None:
                    for t in range(0, TT, 2):
                        evacuate(0, ln1, t)
                if m is not None:
                    act.wait_ge(proj_full, TT * n if n is not None else TT * G * B)
                    for i in range(JT * HALVES):
                        j = i // HALVES
                        act.wait_ge(fc1_full, JT * HALVES * m + i + 1)
                        if i >= 4:
                            act.wait_ge(u_ready, JT * HALVES * m + i - 3)
                        nc.scalar.activation(u_full[:, i % 4, :], tail[:, (i % 2) * N:(i % 2 + 1) * N], ACT.Gelu_apprx_tanh,
                                             bias=fc1_bias[:, j:j + 1]).then_inc(gelu_ready, 1)
                        if ln1 is not None and i % 2:
                            evacuate(0, ln1, i - 1)
                if n is not None:
                    for t in range(TILES):
                        act.wait_ge(neg_max_ready, TILES * n + t + 1)
                        nc.scalar.activation(pair[t % 3][:, :], pair[t % 3][:, :], ACT.Exp, bias=neg_max[:, t:t + 1],
                                             accum_out=den[:, t:t + 1]).then_inc(exp_done, 1)
                    if m is not None:
                        act.wait_ge(fc2_full, TT * (m + 1))
                    for t in range(TILES):
                        kt, h = t // HG, t % HG
                        act.wait_ge(score_t_full, TILES * n + t + 1)
                        if kt >= 2 and h == 0:
                            act.wait_ge(probs_used, HALVES * (TT * n + kt - 1))
                        nc.scalar.activation(probs[:, (kt % 2) * HG + h, :], pair[ring(t) % 3][:, :], ACT.Exp).then_inc(exp_done, 1)

            loops(act, step)
            standard_deviation(1, B - 1)
            for t in range(0, TT, 2):
                evacuate(1, B - 1, t)
            act.wait_ge(h2_ready, TT * B)
            with act.Fori(0, G) as g:
                step(None, g, g + (B - 1) * G, B)

        @block.vector
        def _(dve):
            nc.vector.memset(k_st[STACK:STACK + 3, :, :].bitcast(F32), 1.0).then_inc(stacks_primed, 1)
            dve.wait_ge(silu_exp, 1)
            nc.vector.tensor_scalar(silu[:, :], silu[:, :], 1.0, None, ALU.add).then_inc(silu_step, 1)
            dve.wait_ge(silu_step, 1)
            nc.vector.reciprocal(silu[:, :], silu[:, :]).then_inc(silu_step, 1)
            dve.wait_ge(silu_step, 2)
            nc.vector.tensor_tensor(silu[:, :], silu[:, :], cond[:, :], ALU.mult).then_inc(silu_ready, 1)
            def modulation(which):
                vecs = slice(2 * KT * which, 2 * KT * (which + 1))
                for b in range(B):
                    last = nc.vector.tensor_tensor(mod_all[:, b, vecs],
                                                   tail[:, 0:NMOD * B].rearrange("p (f b) -> p b f", b=B)[:, b, vecs],
                                                   ada_bias[:, vecs], ALU.add)
                last.then_inc(mod_step, 1)
                dve.wait_ge(mod_step, 2 * which + 1)
                sc = mod_all[:, :, (2 * which + 1) * KT:(2 * which + 2) * KT]
                nc.vector.tensor_scalar(sc, sc, 1.0, None, ALU.add).then_inc(mod_step, 1)
                dve.wait_ge(mod_step, 2 * which + 2)

            def gate_row(row):
                nc.vector.tensor_tensor(gate_rows[:, row * C:(row + 1) * C], (tail[0:B, N:2 * N], pair[1][0:B, 0:N])[row],
                                        gate_bias[:, row * C:(row + 1) * C], ALU.add).then_inc(gates_ready, 1)

            def pick_mod(which, b):
                if not known(b, 0):
                    dve.wait_ge(even_out[which], TT // 2 * b)
                vecs = slice(2 * KT * which, 2 * KT * (which + 1))
                nc.vector.tensor_copy(mod[:, vecs], mod_all[:, bass.ds(b, 1), vecs].rearrange("p o f -> p (o f)")).then_inc(mod_ready[which], 1)

            def statistics(which, b):
                for t in range(TT):
                    last = nc.vector.bn_stats(bn6[:, t, :], x_next[:, t, :])
                last.then_inc(norm_step[which], 1)

            def normalize(which, b, dst):
                for t in range(TT):
                    last = nc.vector.bn_aggr(mean_var[:, t, :], bn6[:, t, :])
                last.then_inc(var_ready[which], 1)
                dve.wait_ge(std_ready[which], b + 1)
                nc.vector.reciprocal(rstd[:, :], std[:, :]).then_inc(norm_step[which], 1)
                dve.wait_ge(norm_step[which], 3 * b + 2)
                nc.vector.scalar_tensor_tensor(out=shift[:, :], in0=mean_var[:, :, 0], scalar=-1.0, in1=rstd[:, :],
                                               op0=ALU.mult, op1=ALU.mult).then_inc(norm_step[which], 1)
                dve.wait_ge(norm_step[which], 3 * b + 3)
                for t in range(TT):
                    nc.vector.tensor_scalar(dst[:, t, :], x_next[:, t, :], rstd[:, t:t + 1], shift[:, t:t + 1],
                                            ALU.mult, ALU.add).then_inc(norm_ready[which], 1)

            def evacuate1(b, t):
                dve.wait_ge(norm_t[0], TT * b + t + 1)
                norm_evacuate(False, 0, b, t)

            def evacuate2(b):
                for t in range(TT):
                    if t % 2:
                        if t >= 4:
                            dve.wait_ge(h2_ready, TT * b + t - 3)
                        dve.wait_ge(norm_t[1], TT * b + t + 1)
                        norm_evacuate(False, 1, b, t)
                        dve.wait_ge(odd_out[1], TT // 2 * b + t // 2 + 1)
                    else:
                        dve.wait_ge(even_out[1], TT // 2 * b + t // 2 + 1)
                    nc.vector.tensor_copy(h2_hi[:, :, t * P:(t + 1) * P],
                                          u_full[:, t % 4, :].rearrange("p (k c) -> p k c", c=P)).then_inc(h2_split, 1)

            def gate_sum(acc, gate, gated):
                for t in range(TT):
                    last = nc.vector.tensor_tensor(acc[:, t, :], acc[:, t, :], gate[:, :], ALU.mult)
                last.then_inc(gated, 1)

            def add_residual(acc, ready):
                for t in range(TT):
                    last = nc.vector.tensor_tensor(x_next[:, t, :], x_next[:, t, :], acc[:, t, :], ALU.add)
                last.then_inc(ready, 1)

            def set_q_mask(b):
                dve.wait_ge(mask_loaded, 16 * (b + 1))
                nc.vector.tensor_scalar(q_mask[:, :], mask_u8[:, :], SCALE, None, ALU.mult).then_inc(mask_ready, 1)

            dve.wait_ge(x_loaded, 16)
            statistics(0, 0)
            dve.wait_ge(norm_step[0], 1)
            normalize(0, 0, x_next)
            dve.wait_ge(ada_done, 2)
            modulation(0)
            pick_mod(0, 0)
            dve.wait_ge(mod_ready[0], 1)
            for t in range(1, TT, 2):
                evacuate1(0, t)
            set_q_mask(0)

            def split_high(part, m):
                dve.wait_ge(raw_loaded, 32 * m + 16 * (part + 1))
                for c in range(FC2_W // N):
                    cols = slice(c * N, (c + 1) * N)
                    done = nc.vector.tensor_copy(w_hi[:, cols], w_raw[:, cols])
                if part == 0:
                    done = nc.vector.tensor_copy(fc1_bias[:, :], w_raw[:, FC1_W:FC1_W + JT])
                done.then_inc(w_hi_ready, 1)

            def fc2_add(m, tt):
                dve.wait_ge(fc2_full, TT * m + tt + 1)
                nc.vector.tensor_tensor(mlp_acc[:, tt, :], tail[:, (tt % 2) * N:(tt % 2 + 1) * N], mlp_acc[:, tt, :],
                                        ALU.add).then_inc(fc2_added, 1)

            def scale_q_or_k(n, i, dst, msk, ready):
                for half in range(HALVES):
                    cols = slice(half * N, (half + 1) * N)
                    dve.wait_ge(qkv_full, 3 * HALVES * n + HALVES * i + half + 1)
                    nc.vector.scalar_tensor_tensor(out=dst[:, cols], in0=pair[i][:, cols],
                                                   scalar=w_qkv[:, QKV_W + i:QKV_W + i + 1], in1=msk[:, cols],
                                                   op0=ALU.add, op1=ALU.mult).then_inc(ready, 1)

            def step(n, g, m, b, ln1=None, ln2=None, fin=None):
                if m is not None:
                    split_high(0, m)
                if ln2 is not None:
                    dve.wait_ge(x_again, 32 * b)
                    dve.wait_ge(proj_added, TT * G * b)
                    gate_sum(attn_acc, gate1, x1_gated)
                if known(g, 0):
                    dve.wait_ge(mask_ready, b + 1)
                if n is not None:
                    scale_q_or_k(n, 0, qf, q_mask, q_full_ready)
                if ln2 is not None:
                    dve.wait_ge(x1_gated, b)
                    add_residual(attn_acc, x1_ready)
                    dve.wait_ge(x1_ready, b)
                    statistics(1, ln2)
                    dve.wait_ge(norm_step[1], 3 * ln2 + 1)
                    pick_mod(1, ln2)
                if ln1 is not None:
                    dve.wait_ge(x_loaded, 16 * ln1 + 16)
                    statistics(0, ln1)
                    dve.wait_ge(norm_step[0], 3 * ln1 + 1)
                    pick_mod(0, ln1)
                if n is not None:
                    scale_q_or_k(n, 1, kf, mask_u8, k_full_ready)
                if ln1 is not None:
                    normalize(0, ln1, x_next)
                if ln2 is not None:
                    normalize(1, ln2, attn_acc)
                if n is not None:
                    dve.wait_ge(v_t, n + 1)
                    nc.vector.tensor_copy(v_tok[:, :, :].rearrange("p t c -> p (t c)"), pair[0][:, :]).then_inc(v_ready, 1)
                if ln2 is not None:
                    evacuate2(ln2)
                if known(n, 0):
                    dve.wait_ge(ada_done, 3)
                    gate_row(0)
                    dve.wait_ge(ada_done, 6)
                    gate_row(1)
                    modulation(1)
                if ln1 is not None:
                    dve.wait_ge(mod_ready[0], ln1 + 1)
                    if m is None:
                        for t in range(1, TT, 2):
                            evacuate1(ln1, t)
                if m is not None:
                    if n is not None:
                        dve.wait_ge(stack_loaded, 16 * 6 * HG * (n + 1))
                    for i in range(JT * HALVES):
                        j, half = i // HALVES, i % HALVES
                        dve.wait_ge(gelu_ready, JT * HALVES * m + i + 1)
                        nc.vector.tensor_copy(u_hi[:, j, half * N:(half + 1) * N], u_full[:, i % 4, :]).then_inc(u_hi_ready, 1)
                        if ln1 is not None and i >= 2 and i % 2 == 0:
                            evacuate1(ln1, i - 1)
                    if ln1 is not None:
                        evacuate1(ln1, TT - 1)
                    dve.wait_ge(mlp_acc_loaded, 16 * b)
                    dve.wait_ge(fc1_full, JT * HALVES * (m + 1))
                    split_high(1, m)
                if n is not None:
                    for t in range(TILES):
                        if m is not None and t in fc2_adds:
                            fc2_add(m, fc2_adds[t])
                        dve.wait_ge(score_full, TILES * n + t + 1)
                        nc.vector.tensor_reduce(neg_max[:, t:t + 1], pair[t % 3][:, :], AX_X, ALU.max,
                                                negate=True).then_inc(neg_max_ready, 1)
                    dve.wait_ge(neg_max_ready, TILES * (n + 1))
                    nc.vector.tensor_copy(stat[:, 0:TILES].bitcast(F32R), neg_max[:, :]).then_inc(stat_step, 1)
                    dve.wait_ge(stat_step, n + 1)
                    nc.vector.tensor_tensor(stat[:, TILES:2 * TILES], neg_max[:, :], stat[:, 0:TILES], ALU.subtract)
                    dve.wait_ge(exp_done, 2 * TILES * n + TILES)
                    nc.vector.reciprocal(stat[:, 2 * TILES:3 * TILES], den[:, :]).then_inc(stat_ready, 1)
                if m is not None:
                    for tt in range(0 if n is None else FC2_INSIDE, TT - 2):
                        fc2_add(m, tt)
                if n is not None:
                    dve.wait_ge(stat_turned, n + 1)
                    nc.vector.tensor_copy(stat_t[:, :], pair[2][0:3 * TILES, 0:P]).then_inc(stat_t_ready, 1)
                if m is not None:
                    fc2_add(m, TT - 2)
                    fc2_add(m, TT - 1)
                if ln1 is not None:
                    set_q_mask(ln1)
                if fin is not None:
                    dve.wait_ge(x1_again, 32 * b)
                    dve.wait_ge(fc2_added, TT * G * b)
                    gate_sum(mlp_acc, gate2, mlp_gated)
                if n is not None:
                    dve.wait_ge(den_spread, n + 1)
                    nc.vector.tensor_copy(den_bc[:, :], pair[SPREAD_AT % 3][:, :]).then_inc(den_bc_ready, 1)
                    if fin is not None:
                        dve.wait_ge(mlp_gated, b)
                        add_residual(mlp_acc, final_ready)
                    dve.wait_ge(den_bc_ready, n + 1)
                    for half in range(HALVES):
                        cols = slice(half * N, (half + 1) * N)
                        dve.wait_ge(probs_used, HALVES * TT * n + HALVES * (TT - 1) + half + 1)
                        nc.vector.tensor_tensor(attn_ch[:, cols], tail[:, cols], den_bc[:, cols], ALU.mult).then_inc(attn_ready, 1)
                    dve.wait_ge(acc_loaded, 16 * (b + 1))
                    for tt in range(TT):
                        dve.wait_ge(proj_full, TT * n + tt + 1)
                        nc.vector.tensor_tensor(attn_acc[:, tt, :], pair[PROJ_PAIR[tt // 2]][:, (tt % 2) * N:(tt % 2 + 1) * N],
                                                attn_acc[:, tt, :], ALU.add).then_inc(proj_added, 1)

            loops(dve, step)
            dve.wait_ge(x_again, 32 * B)
            dve.wait_ge(proj_added, TT * G * B)
            gate_sum(attn_acc, gate1, x1_gated)
            dve.wait_ge(x1_gated, B)
            add_residual(attn_acc, x1_ready)
            dve.wait_ge(x1_ready, B)
            statistics(1, B - 1)
            dve.wait_ge(norm_step[1], 3 * B - 2)
            pick_mod(1, B - 1)
            normalize(1, B - 1, attn_acc)
            dve.wait_ge(mod_ready[1], B)
            evacuate2(B - 1)
            with dve.Fori(0, G) as g:
                step(None, g, g + (B - 1) * G, B)
            dve.wait_ge(x1_again, 32 * (B - 1) + 16)
            dve.wait_ge(fc2_added, TT * G * B)
            gate_sum(mlp_acc, gate2, mlp_gated)
            dve.wait_ge(mlp_gated, B)
            add_residual(mlp_acc, final_ready)

        @block.tensor
        def _(pe):
            pe.wait_ge(silu_ready, 1)
            sl = silu[:, :].rearrange("p (k b) -> p k b", b=B)

            def modulate_chunk(i):
                pe.wait_ge(ada_loaded[i], 16)
                if i in (2, 5):
                    dst = tail[0:B, N:2 * N] if i == 2 else pair[1][0:B, 0:N]
                    for k in range(KT):
                        last = nc.tensor.matmul(dst, sl[:, k, :], ada_w[:, i % 4, k, :], start=k == 0, stop=k == KT - 1)
                else:
                    for f in range(KT):
                        col = ((i if i < 2 else i - 1) * KT + f) * B
                        for k in range(KT):
                            last = nc.tensor.matmul(tail[:, col:col + B], ada_w[:, i % 4, k, f * P:(f + 1) * P], sl[:, k, :],
                                                    start=k == 0, stop=k == KT - 1)
                last.then_inc(ada_done, 1)

            def transpose_tile(which, b, t):
                src = x_next if which == 0 else attn_acc
                pe.wait_ge(norm_ready[which], TT * b + t + 1)
                if t >= 4:
                    out_sem = odd_out if t % 2 else even_out
                    pe.wait_ge(out_sem[which], TT // 2 * b + t // 2 - 1)
                for k in range(KT):
                    o = (t // 2 % 2) * N + k * P
                    last = nc.tensor.transpose(pair[1 + t % 2][:, o:o + P], src[:, t, k * P:(k + 1) * P], ident[:, :])
                last.then_inc(norm_t[which], 1)

            modulate_chunk(0)
            modulate_chunk(1)
            pe.wait_ge(consts_ready, 2)
            for t in range(TT):
                transpose_tile(0, 0, t)

            def fc1(m, i):
                j, half = i // HALVES, i % HALVES
                if i >= 2:
                    pe.wait_ge(gelu_ready, JT * HALVES * m + i - 1)
                dst = tail[:, (i % 2) * N:(i % 2 + 1) * N]
                terms = [(w, h) for w, h in ((w_lo, h2_hi), (w_hi, h2_lo), (w_hi, h2_hi))]
                for a, (w, h) in enumerate(terms):
                    for k in range(KT):
                        last = nc.tensor.matmul(dst, w[:, (k * JT + j) * P:(k * JT + j + 1) * P], h[:, k, half * N:(half + 1) * N],
                                                start=a == 0 and k == 0, stop=a == 2 and k == KT - 1)
                last.then_inc(fc1_full, 1)

            def fc2_piece(m, tt, term):
                if term == 0:
                    if tt >= 2:
                        pe.wait_ge(fc2_added, TT * m + tt - 1)
                    else:
                        pe.wait_ge(gelu_ready, JT * HALVES * (m + 1))
                    if tt == 0:
                        pe.wait_ge(u_ready, JT * HALVES * (m + 1))
                        pe.wait_ge(w_hi_ready, 2 * m + 2)
                if tt == 0 and term == 2:
                    pe.wait_ge(w_ready, 2 * m + 2)
                u, w = ((u_lo, w_hi), (u_hi, w_hi), (u_hi, w_lo))[term]
                for j in range(JT):
                    last = nc.tensor.matmul(tail[:, (tt % 2) * N:(tt % 2 + 1) * N], u[:, j, tt * P:(tt + 1) * P],
                                            w[:, j * C:(j + 1) * C], start=term == 0 and j == 0, stop=term == 2 and j == JT - 1)
                if term == 2:
                    last.then_inc(fc2_full, 1)

            def fc2(m, tt):
                for term in range(3):
                    fc2_piece(m, tt, term)

            def step(n, g, m, b, ln1=None, ln2=None, fin=None):
                if n is not None:
                    pe.wait_ge(wqkv_loaded, 16 * (n + 1))
                    pe.wait_ge(even_out[0], TT // 2 * (b + 1))
                    pe.wait_ge(odd_out[0], TT // 2 * (b + 1))
                    for i in range(3):
                        if i == 1 and ln2 is not None:
                            pe.wait_ge(proj_added, TT * G * b)
                        elif i == 1 and not known(n, 0):
                            pe.wait_ge(q_full_ready, HALVES * n + 1)
                        for half in range(HALVES):
                            for k in range(KT):
                                last = nc.tensor.matmul(pair[i][:, half * N:(half + 1) * N], w_qkv[:, (i * KT + k) * P:(i * KT + k + 1) * P],
                                                        h1[:, k, half * N:(half + 1) * N], start=k == 0, stop=k == KT - 1)
                            last.then_inc(qkv_full, 1)
                if m is not None and ln2 is None:
                    pe.wait_ge(w_ready, 2 * m + 1)
                    fc1(m, 0)
                if n is not None:
                    pe.wait_ge(v_ch_ready, HALVES * (n + 1))
                    pe.wait_ge(q_full_ready, HALVES * (n + 1))
                    for t in range(TT):
                        last = nc.tensor.transpose(pair[0][:, t * P:(t + 1) * P], v_ch[:, t * P:(t + 1) * P], ident[:, :])
                    last.then_inc(v_t, 1)
                if known(n, 0):
                    pe.wait_ge(mod_step, 2)
                    for i in range(2, 6):
                        modulate_chunk(i)
                    pe.wait_ge(mod_step, 4)
                    pe.wait_ge(gates_ready, 2)
                if ln2 is not None:
                    pe.wait_ge(k_full_ready, HALVES * (n + 1))
                    for t in range(TT):
                        transpose_tile(1, ln2, t)
                    pe.wait_ge(w_ready, 2 * m + 1)
                    pe.wait_ge(h2_ready, TT * ln2 + TT // 2)
                    fc1(m, 0)
                    pe.wait_ge(h2_ready, TT * b)
                if m is not None:
                    for i in range(1, JT * HALVES):
                        fc1(m, i)
                        if ln1 is not None:
                            if i == 1:
                                pe.wait_ge(k_full_ready, HALVES * (n + 1))
                            transpose_tile(0, ln1, i - 1)
                    if ln1 is not None:
                        transpose_tile(0, ln1, TT - 1)
                elif ln1 is not None:
                    pe.wait_ge(k_full_ready, HALVES * (n + 1))
                    for t in range(TT):
                        transpose_tile(0, ln1, t)
                for which, ln in ((0, ln1), (1, ln2)):
                    if ln is not None:
                        pe.wait_ge(even_out[which], TT // 2 * ln + TT // 2)
                        pe.wait_ge(odd_out[which], TT // 2 * ln + TT // 2)
                if n is not None:
                    pe.wait_ge(stack_loaded, 16 * 6 * HG * (n + 1))
                    pe.wait_ge(mask_rows, 2 * (b + 1))
                    pe.wait_ge(v_ready, n + 1)
                    pe.wait_ge(k_full_ready, HALVES * (n + 1))
                    for t in range(TILES):
                        h, qt = t // TT, t % TT
                        if m is not None:
                            for tt, term in fc2_pieces.get(t, ()):
                                fc2_piece(m, tt, term)
                        if t >= 3:
                            pe.wait_ge(exp_done, 2 * TILES * n + t - 2)
                        for half in range(HALVES):
                            last = nc.tensor.matmul(pair[t % 3][:, half * N:(half + 1) * N], q_st[0:MAX_ROW, h, qt * P:(qt + 1) * P],
                                                    k_st[0:MAX_ROW, h, half * N:(half + 1) * N], start=True, stop=True)
                        last.then_inc(score_full, 1)
                if m is not None:
                    for tt in range(0 if n is None else FC2_INSIDE, TT - 2):
                        fc2(m, tt)
                if n is not None:
                    pe.wait_ge(stat_ready, n + 1)
                    nc.tensor.transpose(pair[2][0:3 * TILES, 0:P], stat[:, :], ident[:, :]).then_inc(stat_turned, 1)
                if m is not None:
                    fc2(m, TT - 2)
                    fc2(m, TT - 1)
                if n is not None:
                    pe.wait_ge(rows_loaded, 16 * (n + 1))
                    pe.wait_ge(stat_t_ready, n + 1)

                    def weigh(kt):
                        pe.wait_ge(exp_done, 2 * TILES * n + TILES + HG * (kt + 1))
                        for half in range(HALVES):
                            for h in range(HG):
                                last = nc.tensor.matmul(tail[h * HD:(h + 1) * HD, half * N:(half + 1) * N],
                                                        v_tok[:, kt, h * HD:(h + 1) * HD],
                                                        probs[:, (kt % 2) * HG + h, half * N:(half + 1) * N],
                                                        start=kt == 0, stop=kt == TT - 1)
                            last.then_inc(probs_used, 1)

                    if m is not None:
                        pe.wait_ge(fc2_added, TT * (m + 1))
                    for kt in range(TT):
                        for h in range(HG):
                            t = kt * HG + h
                            if t == SPREAD_AT:
                                pe.wait_ge(den_loaded, 16 * (n + 1))
                                pe.wait_ge(exp_done, 2 * TILES * n + TILES + t - 2)
                                for half in range(HALVES):
                                    last = nc.tensor.matmul(pair[SPREAD_AT % 3][:, half * N:(half + 1) * N], head_sel[:, :],
                                                            den_row[:, half * N:(half + 1) * N], start=True, stop=True)
                                last.then_inc(den_spread, 1)
                            if ring(t) == SPREAD_AT + 3:
                                pe.wait_ge(den_bc_ready, n + 1)
                            elif t >= 3:
                                pe.wait_ge(exp_done, 2 * TILES * n + TILES + t - (2 if not SPREAD_AT <= t <= SPREAD_AT + 1 else 1))
                            for half in range(HALVES):
                                last = nc.tensor.matmul(pair[ring(t) % 3][:, half * N:(half + 1) * N], k_st[0:MAX_ROW + 2, h, kt * P:(kt + 1) * P],
                                                        q_st[0:MAX_ROW + 2, h, half * N:(half + 1) * N], start=True, stop=True)
                            last.then_inc(score_t_full, 1)
                        if kt:
                            weigh(kt - 1)
                    weigh(TT - 1)
                    pe.wait_ge(wproj_loaded, 16 * (n + 1))
                    for tt in range(TT):
                        pe.wait_ge(attn_ready, HALVES * n + tt // (TT // HALVES) + 1)
                        if tt >= 6:
                            pe.wait_ge(proj_added, TT * n + tt - 3)
                        nc.tensor.matmul(pair[PROJ_PAIR[tt // 2]][:, (tt % 2) * N:(tt % 2 + 1) * N], attn_ch[:, tt * P:(tt + 1) * P],
                                         w_proj[:, :], start=True, stop=True).then_inc(proj_full, 1)
            loops(pe, step)
            pe.wait_ge(proj_added, TT * G * B)
            for t in range(TT):
                transpose_tile(1, B - 1, t)
            pe.wait_ge(h2_ready, TT * B)
            with pe.Fori(0, G) as g:
                step(None, g, g + (B - 1) * G, B)


def kernel(x, cond_1024, mask_BxS_bk1, L0_cond_qkv_w, L0_cond_qkv_b, L0_cond_proj_w, L0_cond_proj_b,
           L0_cond_fc1_w, L0_cond_fc1_b, L0_cond_fc2_w, L0_cond_fc2_b, L0_cond_ada_w, L0_cond_ada_b):
    import numpy as np
    import concourse.bacc as bacc
    from concourse.bass_utils import run_bass_kernel_spmd

    def rows(a):
        return np.ascontiguousarray(a)

    def wrapped(a):
        return np.concatenate([a, a[:1]], axis=0)

    qkv = np.asarray(L0_cond_qkv_w).reshape(3, G, P, KT, P).transpose(1, 4, 0, 3, 2).reshape(G, P, QKV_W)
    qkv_b = np.asarray(L0_cond_qkv_b).reshape(3, G, P).transpose(1, 2, 0)
    fc1 = np.asarray(L0_cond_fc1_w).reshape(G, JT * P, KT, P).transpose(0, 3, 2, 1).reshape(G, P, FC1_W)
    fc1_b = np.asarray(L0_cond_fc1_b).reshape(G, JT, P).transpose(0, 2, 1)
    fc2 = np.asarray(L0_cond_fc2_w).reshape(C, G, JT, P).transpose(1, 3, 2, 0).reshape(G, P, FC2_W)
    ada = np.asarray(L0_cond_ada_w).reshape(6, C, KT, P).transpose(0, 3, 2, 1)
    ada_b = np.asarray(L0_cond_ada_b).reshape(6, KT, P)
    arrays = {
        "x": rows(x),
        "cond_t": rows(np.asarray(cond_1024).reshape(B, KT, P).transpose(2, 1, 0).reshape(P, KT * B)),
        "mask": rows(mask_BxS_bk1),
        "wqkv": rows(wrapped(np.concatenate([qkv, qkv_b], axis=2))),
        "wproj": rows(wrapped(np.asarray(L0_cond_proj_w).T.reshape(G, P, C))),
        "wfc1": rows(wrapped(np.concatenate([fc1, fc1_b], axis=2))),
        "wfc2": rows(fc2),
        "proj_b": rows(np.asarray(L0_cond_proj_b).reshape(1, 1, C)),
        "fc2_b": rows(np.asarray(L0_cond_fc2_b).reshape(1, 1, C)),
        "ada_wt": rows(ada),
        "ada_bt": rows(ada_b[[0, 1, 3, 4]].transpose(2, 0, 1).reshape(P, NMOD)),
        "ada_bg": rows(ada_b[[2, 5]].reshape(1, 2 * C)),
    }
    nc = bacc.Bacc("TRN2", target_bir_lowering=False, num_devices=1, dynamic_dma_scratch_size=1024)
    args = [nc.dram_tensor(f"in_{n}", a.shape, mybir.dt.from_np(a.dtype), kind="ExternalInput").ap() for n, a in arrays.items()]
    out = nc.dram_tensor("out_x", (B, S, C), F32, kind="ExternalOutput").ap()
    block_kernel(nc, *args, out)
    r = run_bass_kernel_spmd(nc, [{f"in_{n}": a for n, a in arrays.items()}], core_ids=[0])
    return r.results[0]["out_x"]
```

```python
from contextlib import ExitStack

import concourse.bass as bass
from concourse import mybir

F32 = mybir.dt.float32
F32R = mybir.dt.float32r
U8 = mybir.dt.uint8
ALU = mybir.AluOpType
ACT = mybir.ActivationFunctionType
AX_X = mybir.AxisListType.X

B, S, C = 4, 1024, 512
HEADS, HD, HIDDEN = 16, 32, 2048
EPS = 1e-6
P = 128
KT = C // P
TT = S // P
G = C // P
HG = HEADS // G
JT = HIDDEN // G // P
N = 512
HALVES = S // N
TILES = HG * TT
STACK = 3 * HD
MASK_ROW = STACK
MAX_ROW = STACK + 1
SCALE = HD ** -0.5
NEG = 1.0e9
QKV_W = 3 * KT * P
FC1_W = KT * JT * P
FC2_W = JT * C
NMOD = 4 * KT
FILL_FIRST = 2
V_FIRST = 8
FC2_INSIDE = 4
PROJ_PAIR = (0, 1, 2, 1)
WEIGH_AFTER = (1, 3)
SPREAD_AT = 7
PROJ_AT = (9, 13, 17, 21)

LAST_STORES = ((0, 4), (4, 6), (6, 7), (7, 8))


def known(index, value):
    return isinstance(index, int) and index == value


def fillers(with_mlp):
    units = [("fc2", 0), ("v", 0), ("fc2", 1), ("v", 1)] + [("fc2", tt) for tt in range(2, FC2_INSIDE)]
    units = [u for u in units if with_mlp or u[0] == "v"]
    pieces = [(what, i, p) for what, i in units for p in range(3 if what == "fc2" else KT)]
    at, due = {}, {}
    first = FILL_FIRST if with_mlp else V_FIRST
    for index, (what, i, p) in enumerate(pieces):
        t = first + index * (TILES - first) // len(pieces)
        at.setdefault(t, []).append((what, i, p))
        due[(what, i)] = min(t + 1, TILES - 1)
    return at, {t: [u for u in units if due[u] == t] for t in due.values()}


def fc2_half(tt):
    return 0 if tt < 2 else tt % 2


def key_major_units(with_proj):
    units = []
    for t in range(TILES):
        if t == SPREAD_AT:
            units.append(("spread", 0))
        if with_proj and t in PROJ_AT:
            units.append(("proj", PROJ_AT.index(t)))
        units.append(("score", t))
    return units


def block_kernel(nc, x, cond_t, mask, wqkv, wproj, wfc1, wfc2, proj_b, fc2_b, ada_wt, ada_bt, ada_bg, out):
    x1_dram = nc.dram_tensor("x1_dram", (B, S, C), F32, kind="Internal").ap()
    gate_dram = nc.dram_tensor("gate_dram", (B, 2 * C), F32, kind="Internal").ap()

    with ExitStack() as ctx:
        def sb(name, shape, dt=F32):
            return ctx.enter_context(nc.sbuf_tensor(name, shape, dt))

        def sem(name):
            return ctx.enter_context(nc.semaphore(name))

        w_qkv = sb("w_qkv", [P, QKV_W + 3])
        w_proj = sb("w_proj", [P, C])
        w_raw = sb("w_raw", [P, FC1_W + JT])
        w_hi = sb("w_hi", [P, FC1_W], F32R)
        w_lo = sb("w_lo", [P, FC1_W], F32R)
        fc1_bias = sb("fc1_bias", [P, JT])
        attn_acc = sb("attn_acc", [P, TT, C])
        x_next = sb("x_next", [P, TT, C])
        mlp_acc = sb("mlp_acc", [P, TT, C])
        h1 = sb("h1", [P, KT, S])
        q_st = sb("q_st", [P, HG, S], F32R)
        k_st = sb("k_st", [P, HG, S], F32R)
        v_tok = sb("v_tok", [P, TT, P])
        attn_ch = sb("attn_ch", [P, S])
        mask_u8 = sb("mask_u8", [P, S], U8)
        gate1 = sb("gate1", [P, C])
        gate2 = sb("gate2", [P, C])
        den_row = sb("den_row", [2 * HG, S], F32R)
        ident = sb("ident", [P, P])
        head_ones = sb("head_ones", [2 * HG, P])
        head_sel = sb("head_sel", [2 * HG, P], F32R)
        neg_max = sb("neg_max", [P, TILES])
        den = sb("den", [P, TILES])
        inv_den = sb("inv_den", [P, TILES])
        stat = sb("stat", [P, 4 * TILES])
        stat_t = sb("stat_t", [4 * TILES, P])
        mod_all = sb("mod_all", [P, B, NMOD])
        mod = sb("mod", [P, NMOD])
        eps_col = sb("eps_col", [P, 1])
        bn6 = sb("bn6", [P, TT, 6])
        mean_var = sb("mean_var", [P, TT, 2])
        std = sb("std", [P, TT])
        rstd = sb("rstd", [P, TT])
        shift = sb("shift", [P, TT])
        ada_bias = sb("ada_bias", [P, NMOD])
        cond = sb("cond", [P, KT * B])
        silu = sb("silu", [P, KT * B])

        def in_turn(*layouts):
            made = []
            for layout in layouts:
                with ExitStack() as turn:
                    made.append([turn.enter_context(nc.sbuf_tensor(n, s, d)) for n, s, d in layout])
            return made

        (h2_hi, h2_lo), (ada_w,) = in_turn(
            [("h2_hi", [P, KT, S], F32R), ("h2_lo", [P, KT, S], F32R)],
            [("ada_w", [P, 4, KT, C], F32)],
        )
        ctx.enter_context(nc.sbuf_tensor("h2_region", [P, 2 * KT * S], F32))
        big = in_turn(
            [("u_hi", [P, JT, S], F32R), ("u_lo", [P, JT, S], F32R)],
            [("probs", [P, 2 * HG, S], F32)],
            [("qf", [P, S], F32), ("kf", [P, S], F32), ("q_hi", [P, S], F32R), ("q_lo", [P, S], F32R),
             ("k_hi", [P, S], F32R), ("k_lo", [P, S], F32R)],
        )
        (u_hi, u_lo), (probs,), (qf, kf, q_hi, q_lo, k_hi, k_lo) = big
        ctx.enter_context(nc.sbuf_tensor("big_region", [P, 2 * HG * S], F32))
        (gate_bias, gate_rows), (u_full,), (den_bc, v_ch) = in_turn(
            [("gate_bias", [B, 2 * C], F32), ("gate_rows", [B, 2 * C], F32)],
            [("u_full", [P, 4, N], F32)],
            [("den_bc", [P, S], F32), ("v_ch", [P, S], F32)],
        )
        ctx.enter_context(nc.sbuf_tensor("small_region", [P, 2 * S], F32))

        pair = [ctx.enter_context(nc.psum_tensor(f"pair{i}", [P, S], F32)) for i in range(3)]
        tail = ctx.enter_context(nc.psum_tensor("tail", [P, S], F32))

        consts_ready = sem("consts_ready")
        ident_zero = sem("ident_zero")
        stacks_primed = sem("stacks_primed")
        small_loaded = sem("small_loaded")
        ada_loaded = [sem(f"ada_loaded{i}") for i in range(6)]
        silu_step = sem("silu_step")
        silu_exp = sem("silu_exp")
        silu_ready = sem("silu_ready")
        ada_done = sem("ada_done")
        gates_ready = sem("gates_ready")
        mod_step = sem("mod_step")
        gates_stored = sem("gates_stored")
        x_loaded = sem("x_loaded")
        mask_loaded = sem("mask_loaded")
        mask_rows = sem("mask_rows")
        mod_ready = [sem("mod1_ready"), sem("mod2_ready")]
        acc_loaded = sem("acc_loaded")
        var_ready = [sem("var1_ready"), sem("var2_ready")]
        std_ready = [sem("std1_ready"), sem("std2_ready")]
        norm_ready = [sem("norm1_ready"), sem("norm2_ready")]
        norm_t = [sem("norm1_t"), sem("norm2_t")]
        even_out = [sem("even1_out"), sem("even2_out")]
        odd_out = [sem("odd1_out"), sem("odd2_out")]
        norm_step = [sem("norm1_step"), sem("norm2_step")]
        x1_gated = sem("x1_gated")
        mlp_gated = sem("mlp_gated")
        h2_split = sem("h2_split")
        h2_ready = sem("h2_ready")
        x_again = sem("x_again")
        x1_ready = sem("x1_ready")
        x1_stored = sem("x1_stored")
        x1_again = sem("x1_again")
        final_ready = sem("final_ready")
        out_stored = sem("out_stored")
        mlp_acc_loaded = sem("mlp_acc_loaded")
        wqkv_loaded = sem("wqkv_loaded")
        wproj_loaded = sem("wproj_loaded")
        wq_scaled = sem("wq_scaled")
        qkv_full = sem("qkv_full")
        q_full_ready = sem("q_full_ready")
        k_full_ready = sem("k_full_ready")
        q_hi_ready = sem("q_hi_ready")
        k_hi_ready = sem("k_hi_ready")
        q_lo_ready = sem("q_lo_ready")
        k_lo_ready = sem("k_lo_ready")
        v_full = sem("v_full")
        v_ch_ready = sem("v_ch_ready")
        v_t = sem("v_t")
        v_ready = sem("v_ready")
        stack_loaded = [sem(f"stack_loaded{h}") for h in range(HG)]
        score_full = sem("score_full")
        neg_max_ready = sem("neg_max_ready")
        exp_done = sem("exp_done")
        stat_step = sem("stat_step")
        stat_ready = sem("stat_ready")
        stat_turned = sem("stat_turned")
        stat_t_ready = sem("stat_t_ready")
        rows_loaded = sem("rows_loaded")
        den_loaded = sem("den_loaded")
        score_t_full = sem("score_t_full")
        probs_used = sem("probs_used")
        den_spread = sem("den_spread")
        den_bc_ready = sem("den_bc_ready")
        attn_ready = sem("attn_ready")
        proj_full = sem("proj_full")
        proj_added = sem("proj_added")
        raw_loaded = sem("raw_loaded")
        w_hi_ready = sem("w_hi_ready")
        w_ready = sem("w_ready")
        fc1_full = sem("fc1_full")
        gelu_ready = sem("gelu_ready")
        u_hi_ready = sem("u_hi_ready")
        u_ready = sem("u_ready")
        fc2_full = sem("fc2_full")
        fc2_added = sem("fc2_added")

        block = ctx.enter_context(nc.Block())

        def token_tiles(part):
            return slice(0, TT) if part is None else slice(part * TT // 2, (part + 1) * TT // 2)

        def row_block(dram, b):
            return dram[bass.ds(b, 1)].rearrange("o (t p) c -> p (o t) c", p=P)

        w2_hi = q_st[:, 0:HG // 2, :].rearrange("p h s -> p (h s)")
        w2_lo = q_st[:, HG // 2:HG, :].rearrange("p h s -> p (h s)")

        def norm_place(which, t):
            if which == 1 and t < TT // 2:
                return (tail, pair[0])[t // 2], (t % 2) * N
            return pair[1 + t % 2], (t // 2 % 2) * N

        def fc_weights(part, alone):
            return (w2_hi, w2_lo) if part and alone else (w_hi, w_lo)

        def place(units, what, i):
            return pair[units.index((what, i)) % 3]

        def at(dram, i):
            return dram[bass.ds(i, 1)].rearrange("o p c -> (o p) c")

        def loops(eng, step):
            step(0, 0, None, 0)
            with eng.Fori(1, G - 1) as g:
                step(g, g, None, 0)
            step(G - 1, G - 1, None, 0, ln1=1)

            def batch(b, ln1):
                step(b * G, 0, b * G - G, b, ln2=b - 1)
                with eng.Fori(1, G - 1) as g:
                    step(b * G + g, g, b * G + g - G, b)
                step(b * G + G - 1, G - 1, b * G - 1, b, ln1=ln1, fin=b - 1)

            with eng.Fori(1, B - 1) as b:
                batch(b, b + 1)
            batch(B - 1, None)

        @block.sync
        def _(sp):
            sp.dma_start(cond[:, :], cond_t).then_inc(small_loaded, 16)
            sp.dma_start(ada_bias[:, :], ada_bt).then_inc(small_loaded, 16)
            sp.dma_start(gate_bias[:, :], ada_bg.broadcast_to((B, 2 * C))).then_inc(small_loaded, 16)
            sp.dma_start(x_next[:, :, :], row_block(x, 0)).then_inc(x_loaded, 16)
            for i in range(2):
                sp.dma_start(ada_w[:, i], ada_wt[i]).then_inc(ada_loaded[i], 16)
            sp.dma_start(mask_u8[:, :], mask[0:1].broadcast_to((P, S))).then_inc(mask_loaded, 16)
            sp.dma_start(w_qkv[:, :], at(wqkv, 0)).then_inc(wqkv_loaded, 16)
            for i in range(2, 4):
                sp.dma_start(ada_w[:, i], ada_wt[i]).then_inc(ada_loaded[i], 16)
            sp.wait_ge(ada_done, 2)
            for i in range(4, 6):
                sp.dma_start(ada_w[:, i - 4], ada_wt[i]).then_inc(ada_loaded[i], 16)
            sp.dma_start(w_proj[:, :], at(wproj, 0)).then_inc(wproj_loaded, 16)
            sp.dma_start(attn_acc[:, :, :], proj_b.broadcast_to((P, TT, C))).then_inc(acc_loaded, 16)
            sp.dma_start(w_raw[:, :], at(wfc1, 0)).then_inc(raw_loaded, 16)
            sp.dma_start(mlp_acc[:, :, :], fc2_b.broadcast_to((P, TT, C))).then_inc(mlp_acc_loaded, 16)

            def stack_rows(src, st, part, h):
                sp.dma_start(st[part * HD:(part + 1) * HD, h, :].bitcast(F32),
                             src[h * HD:(h + 1) * HD, :].bitcast(F32)).then_inc(stack_loaded[h], 16)

            def stack_q(n):
                sp.wait_ge(q_hi_ready, n + 1)
                for part in (0, 1):
                    for h in range(HG):
                        stack_rows(q_hi, q_st, part, h)
                sp.wait_ge(q_lo_ready, n + 1)
                for h in range(HG):
                    stack_rows(q_lo, q_st, 2, h)

            def stack_k(n):
                sp.wait_ge(k_hi_ready, n + 1)
                for h in range(HG):
                    stack_rows(k_hi, k_st, 0, h)
                    stack_rows(k_hi, k_st, 2, h)
                    if h == 0:
                        sp.wait_ge(k_lo_ready, n + 1)
                    stack_rows(k_lo, k_st, 1, h)

            def load_fc2(m, g):
                sp.wait_ge(w_ready, 2 * m + 1)
                sp.dma_start(w_raw[:, 0:FC2_W], at(wfc2, g)).then_inc(raw_loaded, 16)

            def load_next_fc1(m, g):
                sp.wait_ge(w_ready, 2 * m + 2)
                sp.dma_start(w_raw[:, :], at(wfc1, g + 1 if not known(g, G - 1) else 0)).then_inc(raw_loaded, 16)

            def step(n, g, m, b, ln1=None, ln2=None, fin=None):
                last_batch = known(b, B - 1)
                if m is not None:
                    load_fc2(m, g)
                stack_q(n)
                if ln2 is not None:
                    sp.wait_ge(x1_ready, 2 * b)
                    sp.dma_start(row_block(x1_dram, ln2), x_next[:, :, :]).then_inc(x1_stored, 16)
                stack_k(n)
                if ln1 is not None:
                    sp.dma_start(mask_u8[:, :], mask[bass.ds(ln1, 1)].broadcast_to((P, S))).then_inc(mask_loaded, 16)
                sp.wait_ge(v_ch_ready, HALVES * (n + 1))
                sp.dma_start(w_qkv[:, :], at(wqkv, g + 1)).then_inc(wqkv_loaded, 16)
                if ln2 is not None:
                    sp.wait_ge(h2_ready, TT * b)
                    sp.dma_start(attn_acc[:, :, :], proj_b.broadcast_to((P, TT, C))).then_inc(acc_loaded, 16)
                if ln1 is not None:
                    sp.wait_ge(norm_t[0], TT * ln1 + TT)
                if fin is not None:
                    sp.dma_start(x_next[:, :, :], row_block(x1_dram, fin)).then_inc(x1_again, 16)
                    sp.dma_start(gate2[:, :], gate_dram[bass.ds(fin, 1), C:2 * C].broadcast_to((P, C))).then_inc(x1_again, 16)
                if m is not None:
                    load_next_fc1(m, g)
                if known(n, 0):
                    sp.wait_ge(gates_ready, 2)
                    sp.dma_start(gate_dram, gate_rows[:, :]).then_inc(gates_stored, 16)
                    sp.wait_ge(gates_stored, 16)
                    sp.wait_ge(norm_t[0], TT)
                    sp.dma_start(x_next[:, :, :], row_block(x, 1)).then_inc(x_loaded, 16)
                sp.wait_ge(stat_t_ready, n + 1)
                sp.dma_start(q_st[MAX_ROW:MAX_ROW + 2, :, :].bitcast(F32).rearrange("r h (t j) -> r (h t) j", j=P),
                             stat_t[0:2 * TILES, :]).then_inc(rows_loaded, 16)
                sp.dma_start(den_row[:, :].bitcast(F32).rearrange("h (t j) -> h t j", j=P),
                             stat_t[2 * TILES:4 * TILES, :]).then_inc(den_loaded, 16)
                if ln2 is not None:
                    sp.wait_ge(x1_stored, 16 * b)
                    if not last_batch:
                        sp.dma_start(x_next[:, :, :], row_block(x, b + 1)).then_inc(x_loaded, 16)
                if fin is not None:
                    sp.wait_ge(final_ready, b)
                    sp.dma_start(row_block(out, fin), x_next[:, :, :]).then_inc(out_stored, 16)
                    sp.dma_start(mlp_acc[:, :, :], fc2_b.broadcast_to((P, TT, C))).then_inc(mlp_acc_loaded, 16)
                    sp.wait_ge(out_stored, 16 * b)
                if known(g, G - 1):
                    sp.dma_start(x_next[:, :, :], row_block(x, b)).then_inc(x_again, 16)
                    sp.dma_start(gate1[:, :], gate_dram[bass.ds(b, 1), 0:C].broadcast_to((P, C))).then_inc(x_again, 16)
                if not known(g, 0):
                    sp.wait_ge(proj_full, TT * n)
                    sp.dma_start(w_proj[:, :], at(wproj, g)).then_inc(wproj_loaded, 16)
                if known(g, G - 1) and not last_batch:
                    sp.wait_ge(proj_full, TT * (n + 1))
                    sp.dma_start(w_proj[:, :], at(wproj, 0)).then_inc(wproj_loaded, 16)

            loops(sp, step)
            sp.dma_start(gate2[:, :], gate_dram[B - 1:B, C:2 * C].broadcast_to((P, C))).then_inc(x1_again, 16)
            load_fc2((B - 1) * G, 0)
            with sp.Fori(0, G - 1) as g:
                m = g + (B - 1) * G
                sp.wait_ge(w_ready, 2 * m + 2)
                sp.dma_start(w_raw[:, :], at(wfc1, g + 1)).then_inc(raw_loaded, 16)
                load_fc2(m + 1, g + 1)
            for first, end in LAST_STORES:
                sp.wait_ge(final_ready, B - 1 + end)
                sp.dma_start(row_block(out, B - 1)[:, first:end, :], x_next[:, first:end, :]).then_inc(out_stored, 16)
            sp.wait_ge(wqkv_loaded, 16 * (B * G + 1))
            sp.wait_ge(wproj_loaded, 16 * B * G)
            sp.wait_ge(raw_loaded, 16 * 2 * B * G)
            sp.wait_ge(acc_loaded, 16 * B)
            sp.wait_ge(x1_stored, 16 * (B - 1))
            sp.wait_ge(out_stored, 16 * (B - 1 + len(LAST_STORES)))

        @block.gpsimd
        def _(pool):
            nc.gpsimd.memset(ident[:, :], 0.0).then_inc(ident_zero, 1)
            nc.gpsimd.memset(head_ones[:, :], 0.0).then_inc(ident_zero, 1)
            nc.gpsimd.memset(eps_col[:, :], EPS).then_inc(ident_zero, 1)
            pool.wait_ge(ident_zero, 3)
            nc.gpsimd.affine_select(out=ident[:, :], in_=ident[:, :], compare_op=ALU.not_equal, fill=1.0,
                                    base=0, pattern=[[-1, P]], channel_multiplier=1).then_inc(consts_ready, 1)
            sel = head_ones[:, :].rearrange("p (h d) -> p h d", d=HD)
            nc.gpsimd.affine_select(out=sel, in_=sel, compare_op=ALU.not_equal, fill=1.0,
                                    base=0, pattern=[[-1, HG], [0, HD]], channel_multiplier=1).then_inc(ident_zero, 1)
            pool.wait_ge(ident_zero, 4)
            nc.gpsimd.affine_select(out=sel, in_=sel, compare_op=ALU.not_equal, fill=1.0,
                                    base=-HG, pattern=[[-1, HG], [0, HD]], channel_multiplier=1).then_inc(ident_zero, 1)
            pool.wait_ge(ident_zero, 5)
            nc.gpsimd.tensor_copy(head_sel[:, :], head_ones[:, :]).then_inc(consts_ready, 1)

            def split_low(part, m, alone=False):
                hi, lo = fc_weights(part, alone)
                pool.wait_ge(w_hi_ready, 2 * m + part + 1)
                for c in range(FC2_W // N):
                    cols = slice(c * N, (c + 1) * N)
                    done = nc.gpsimd.tensor_tensor(lo[:, cols], w_raw[:, cols], hi[:, cols].bitcast(F32), ALU.subtract)
                done.then_inc(w_ready, 1)

            def u_low(m):
                for i in range(JT * HALVES):
                    j, half = i % JT, i // JT
                    cols = slice(half * N, (half + 1) * N)
                    pool.wait_ge(u_hi_ready, JT * HALVES * m + i + 1)
                    nc.gpsimd.tensor_tensor(u_lo[:, j, cols], u_full[:, i % 4, :], u_hi[:, j, cols].bitcast(F32),
                                            ALU.subtract).then_inc(u_ready, 1)

            def h2_low(b, part):
                for t in range(TT)[token_tiles(part)]:
                    pool.wait_ge(h2_split, TT * b + t + 1)
                    cols = slice(t * P, (t + 1) * P)
                    nc.gpsimd.tensor_tensor(h2_lo[:, :, cols], attn_acc[:, t, :].rearrange("p (k c) -> p k c", c=P),
                                            h2_hi[:, :, cols].bitcast(F32), ALU.subtract).then_inc(h2_ready, 1)

            def step(n, g, m, b, ln1=None, ln2=None, fin=None):
                if m is not None:
                    split_low(0, m)
                pool.wait_ge(q_hi_ready, n + 1)
                nc.gpsimd.tensor_tensor(q_lo[:, :], qf[:, :], q_hi[:, :].bitcast(F32), ALU.subtract).then_inc(q_lo_ready, 1)
                if ln2 is not None:
                    h2_low(ln2, 0)
                pool.wait_ge(k_hi_ready, n + 1)
                nc.gpsimd.tensor_tensor(k_lo[:, :], kf[:, :], k_hi[:, :].bitcast(F32), ALU.subtract).then_inc(k_lo_ready, 1)
                if ln2 is not None:
                    h2_low(ln2, 1)
                if m is not None:
                    u_low(m)
                    split_low(1, m)

            loops(pool, step)
            m = (B - 1) * G
            split_low(0, m)
            h2_low(B - 1, 0)
            h2_low(B - 1, 1)
            split_low(1, m, alone=True)
            with pool.Fori(0, G - 1) as g:
                m = g + (B - 1) * G
                u_low(m)
                split_low(0, m + 1, alone=True)
                split_low(1, m + 1, alone=True)
            u_low(B * G - 1)

        def norm_evacuate(eng_is_act, which, b, t):
            for k in range(KT):
                src, o = norm_place(which, t)
                src = src[:, o + k * P:o + (k + 1) * P]
                dst = h1[:, k, t * P:(t + 1) * P] if which == 0 else attn_acc[:, t, k * P:(k + 1) * P]
                sh = mod[:, 2 * KT * which + k:2 * KT * which + k + 1]
                sc = mod[:, 2 * KT * which + KT + k:2 * KT * which + KT + k + 1]
                if eng_is_act:
                    done = nc.scalar.activation(dst, src, ACT.Identity, bias=sh, scale=sc)
                else:
                    done = nc.vector.tensor_scalar(dst, src, sc, sh, ALU.mult, ALU.add)
            done.then_inc((odd_out if t % 2 else even_out)[which], 1)

        @block.scalar
        def _(act):
            act.wait_ge(small_loaded, 48)
            nc.scalar.activation(silu[:, :], cond[:, :], ACT.Exp, scale=-1.0).then_inc(silu_exp, 1)

            def standard_deviation(which, b, part=None):
                ts = token_tiles(part)
                act.wait_ge(var_ready[which], b + 1 if part is None else 2 * b + part + 1)
                nc.scalar.activation(std[:, ts], mean_var[:, ts, 1], ACT.Sqrt, bias=eps_col[:, 0:1]).then_inc(std_ready[which], 1)

            def v_out(n, half):
                act.wait_ge(v_full, HALVES * n + half + 1)
                nc.scalar.activation(v_ch[:, half * N:(half + 1) * N], tail[:, N:2 * N], ACT.Identity,
                                     bias=w_qkv[:, QKV_W + 2:QKV_W + 3]).then_inc(v_ch_ready, 1)

            def norm2_first_half(b):
                standard_deviation(1, b, 0)
                for t in range(TT // 2):
                    evacuate(1, b, t)
                    act.wait_ge((odd_out if t % 2 else even_out)[1], TT // 2 * b + t // 2 + 1)
                    nc.scalar.activation(h2_hi[:, :, t * P:(t + 1) * P],
                                         attn_acc[:, t, :].rearrange("p (k c) -> p k c", c=P), ACT.Copy).then_inc(h2_split, 1)

            def gelus(m, src, ln1=None, ln2=None):
                for i in range(JT * HALVES):
                    j = i % JT
                    act.wait_ge(fc1_full, JT * HALVES * m + i + 1)
                    if i >= 4:
                        act.wait_ge(u_ready, JT * HALVES * m + i - 3)
                    nc.scalar.activation(u_full[:, i % 4, :], src[:, (i % 2) * N:(i % 2 + 1) * N], ACT.Gelu_apprx_tanh,
                                         bias=fc1_bias[:, j:j + 1]).then_inc(gelu_ready, 1)
                    if ln1 is not None and i % 2:
                        evacuate(0, ln1, i - 1)
                    if ln2 is not None and i == 0:
                        for t in range(TT // 2, TT, 2):
                            evacuate(1, ln2, t)

            def fc2_high(m, alone=False):
                act.wait_ge(raw_loaded, 32 * m + 32)
                nc.scalar.activation(fc_weights(1, alone)[0][:, :], w_raw[:, 0:FC2_W], ACT.Copy).then_inc(w_hi_ready, 1)

            def evacuate(which, b, t):
                if t == 0:
                    act.wait_ge(mod_ready[which], b + 1)
                act.wait_ge(norm_t[which], TT * b + t + 1)
                norm_evacuate(True, which, b, t)

            def set_mask_rows(b):
                act.wait_ge(mask_loaded, 16 * (b + 1))
                act.wait_ge(stacks_primed, 1)
                row = mask_u8[MASK_ROW:MASK_ROW + 1, :].unsqueeze(1).broadcast_to((1, HG, S))
                nc.scalar.activation(k_st[MASK_ROW:MASK_ROW + 1, :, :], row, ACT.Copy, scale=NEG, bias=-NEG).then_inc(mask_rows, 1)
                nc.scalar.activation(q_st[MASK_ROW:MASK_ROW + 1, :, :], row, ACT.Copy).then_inc(mask_rows, 1)

            act.wait_ge(consts_ready, 2)
            standard_deviation(0, 0)
            set_mask_rows(0)
            for t in range(0, TT, 2):
                evacuate(0, 0, t)
            for half in range(HALVES):
                v_out(0, half)

            def step(n, g, m, b, ln1=None, ln2=None, fin=None):
                if ln2 is not None:
                    set_mask_rows(b)
                act.wait_ge(q_full_ready, HALVES * (n + 1))
                nc.scalar.activation(q_hi[:, :], qf[:, :], ACT.Copy).then_inc(q_hi_ready, 1)
                if ln2 is not None:
                    norm2_first_half(ln2)
                act.wait_ge(k_full_ready, HALVES * (n + 1))
                nc.scalar.activation(k_hi[:, :], kf[:, :], ACT.Copy).then_inc(k_hi_ready, 1)
                if ln1 is not None:
                    standard_deviation(0, ln1)
                if ln2 is not None:
                    standard_deviation(1, ln2, 1)
                if ln1 is not None and m is None:
                    for t in range(0, TT, 2):
                        evacuate(0, ln1, t)
                if m is not None:
                    act.wait_ge(attn_ready, HALVES * n)
                    act.wait_ge(v_t, n + 1)
                    gelus(m, tail, ln1, ln2)
                    fc2_high(m)
                more = not (known(b, B - 1) and known(g, G - 1))
                due = fillers(m is not None)[1]
                if known(n, 0):
                    act.wait_ge(gates_stored, 16)
                if m is not None and more:
                    act.wait_ge(u_ready, JT * HALVES * (m + 1))
                for t in range(TILES):
                    for what, half in due.get(t, ()):
                        if what == "v" and more:
                            v_out(n + 1, half)
                    act.wait_ge(neg_max_ready, TILES * n + t + 1)
                    nc.scalar.activation(pair[t % 3][:, :], pair[t % 3][:, :], ACT.Exp, bias=neg_max[:, t:t + 1],
                                         accum_out=den[:, t:t + 1]).then_inc(exp_done, 1)
                if m is not None:
                    act.wait_ge(fc2_full, TT * (m + 1))
                units = key_major_units(not known(g, 0))
                for t in range(TILES):
                    kt, h = t // HG, t % HG
                    act.wait_ge(score_t_full, TILES * n + t + 1)
                    if kt >= 2 and h == 0:
                        act.wait_ge(probs_used, HALVES * (TT * n + kt - 1))
                    nc.scalar.activation(probs[:, (kt % 2) * HG + h, :], place(units, "score", t)[:, :], ACT.Exp).then_inc(exp_done, 1)

            loops(act, step)
            norm2_first_half(B - 1)
            standard_deviation(1, B - 1, 1)
            for t in range(TT // 2, TT, 2):
                evacuate(1, B - 1, t)
            fc2_high((B - 1) * G, alone=True)
            with act.Fori(0, G - 1) as g:
                m = g + (B - 1) * G
                gelus(m, pair[0])
                act.wait_ge(fc2_full, TT * (m + 1))
                fc2_high(m + 1, alone=True)
            gelus(B * G - 1, pair[0])

        @block.vector
        def _(dve):
            nc.vector.memset(k_st[STACK:STACK + 3, :, :].bitcast(F32), 1.0).then_inc(stacks_primed, 1)
            dve.wait_ge(silu_exp, 1)
            nc.vector.tensor_scalar(silu[:, :], silu[:, :], 1.0, None, ALU.add).then_inc(silu_step, 1)
            dve.wait_ge(silu_step, 1)
            nc.vector.reciprocal(silu[:, :], silu[:, :]).then_inc(silu_step, 1)
            dve.wait_ge(silu_step, 2)
            nc.vector.tensor_tensor(silu[:, :], silu[:, :], cond[:, :], ALU.mult).then_inc(silu_ready, 1)
            def modulation(which):
                vecs = slice(2 * KT * which, 2 * KT * (which + 1))
                for b in range(B):
                    last = nc.vector.tensor_tensor(mod_all[:, b, vecs],
                                                   tail[:, 0:NMOD * B].rearrange("p (f b) -> p b f", b=B)[:, b, vecs],
                                                   ada_bias[:, vecs], ALU.add)
                last.then_inc(mod_step, 1)
                dve.wait_ge(mod_step, 2 * which + 1)
                sc = mod_all[:, :, (2 * which + 1) * KT:(2 * which + 2) * KT]
                nc.vector.tensor_scalar(sc, sc, 1.0, None, ALU.add).then_inc(mod_step, 1)
                dve.wait_ge(mod_step, 2 * which + 2)

            def gate_row(row):
                nc.vector.tensor_tensor(gate_rows[:, row * C:(row + 1) * C], (tail[0:B, N:2 * N], pair[1][0:B, 0:N])[row],
                                        gate_bias[:, row * C:(row + 1) * C], ALU.add).then_inc(gates_ready, 1)

            def pick_mod(which, b):
                if not known(b, 0):
                    dve.wait_ge(even_out[which], TT // 2 * b)
                vecs = slice(2 * KT * which, 2 * KT * (which + 1))
                nc.vector.tensor_copy(mod[:, vecs], mod_all[:, bass.ds(b, 1), vecs].rearrange("p o f -> p (o f)")).then_inc(mod_ready[which], 1)

            def statistics(which, part=None):
                ts = range(TT)[token_tiles(part)]
                for t in ts:
                    last = nc.vector.bn_stats(bn6[:, t, :], x_next[:, t, :])
                last.then_inc(norm_step[which], 1)

            def normalize(which, b, dst, part=None):
                ts = token_tiles(part)
                index = b if part is None else 2 * b + part
                done = 3 * index
                for t in range(TT)[ts]:
                    last = nc.vector.bn_aggr(mean_var[:, t, :], bn6[:, t, :])
                last.then_inc(var_ready[which], 1)
                dve.wait_ge(std_ready[which], index + 1)
                nc.vector.reciprocal(rstd[:, ts], std[:, ts]).then_inc(norm_step[which], 1)
                dve.wait_ge(norm_step[which], done + 2)
                nc.vector.scalar_tensor_tensor(out=shift[:, ts], in0=mean_var[:, ts, 0], scalar=-1.0, in1=rstd[:, ts],
                                               op0=ALU.mult, op1=ALU.mult).then_inc(norm_step[which], 1)
                dve.wait_ge(norm_step[which], done + 3)
                for t in range(TT)[ts]:
                    nc.vector.tensor_scalar(dst[:, t, :], x_next[:, t, :], rstd[:, t:t + 1], shift[:, t:t + 1],
                                            ALU.mult, ALU.add).then_inc(norm_ready[which], 1)

            def evacuate1(b, t):
                dve.wait_ge(norm_t[0], TT * b + t + 1)
                norm_evacuate(False, 0, b, t)

            def x1_and_statistics(b, part):
                dve.wait_ge(x1_gated, 2 * b + part + 1)
                add_residual(attn_acc, x1_ready, part)
                dve.wait_ge(x1_ready, 2 * b + part + 1)
                statistics(1, part)
                dve.wait_ge(norm_step[1], 6 * b + 3 * part + 1)

            def evacuate2(b):
                dve.wait_ge(h2_split, TT * b + TT // 2)
                for t in range(TT // 2, TT):
                    if t % 2:
                        dve.wait_ge(norm_t[1], TT * b + t + 1)
                        norm_evacuate(False, 1, b, t)
                        dve.wait_ge(odd_out[1], TT // 2 * b + t // 2 + 1)
                    else:
                        dve.wait_ge(even_out[1], TT // 2 * b + t // 2 + 1)
                    nc.vector.tensor_copy(h2_hi[:, :, t * P:(t + 1) * P],
                                          attn_acc[:, t, :].rearrange("p (k c) -> p k c", c=P)).then_inc(h2_split, 1)

            def gate_sum(acc, gate, gated, part=None):
                for t in range(TT)[token_tiles(part)]:
                    last = nc.vector.tensor_tensor(acc[:, t, :], acc[:, t, :], gate[:, :], ALU.mult)
                last.then_inc(gated, 1)

            def add_residual(acc, ready, part=None):
                for t in range(TT)[token_tiles(part)]:
                    last = nc.vector.tensor_tensor(x_next[:, t, :], x_next[:, t, :], acc[:, t, :], ALU.add)
                if ready is not None:
                    last.then_inc(ready, 1)

            def scale_q_weights(n):
                dve.wait_ge(wqkv_loaded, 16 * n + 16)
                for cols in (slice(0, KT * P), slice(QKV_W, QKV_W + 1)):
                    nc.vector.tensor_scalar(w_qkv[:, cols], w_qkv[:, cols], SCALE, None, ALU.mult).then_inc(wq_scaled, 1)

            dve.wait_ge(x_loaded, 16)
            statistics(0)
            dve.wait_ge(norm_step[0], 1)
            normalize(0, 0, x_next)
            dve.wait_ge(ada_done, 2)
            modulation(0)
            pick_mod(0, 0)
            dve.wait_ge(mod_ready[0], 1)
            for t in range(1, TT, 2):
                evacuate1(0, t)
            scale_q_weights(0)

            def fc1_high(m):
                dve.wait_ge(raw_loaded, 32 * m + 16)
                for c in range(FC1_W // N):
                    cols = slice(c * N, (c + 1) * N)
                    nc.vector.tensor_copy(w_hi[:, cols], w_raw[:, cols])
                nc.vector.tensor_copy(fc1_bias[:, :], w_raw[:, FC1_W:FC1_W + JT]).then_inc(w_hi_ready, 1)

            def u_high(m, ln1=None):
                for i in range(JT * HALVES):
                    j, half = i % JT, i // JT
                    dve.wait_ge(gelu_ready, JT * HALVES * m + i + 1)
                    nc.vector.tensor_copy(u_hi[:, j, half * N:(half + 1) * N], u_full[:, i % 4, :]).then_inc(u_hi_ready, 1)
                    if ln1 is not None and i >= 2 and i % 2 == 0:
                        evacuate1(ln1, i - 1)
                if ln1 is not None:
                    evacuate1(ln1, TT - 1)

            def add_projection(tiles, n, b, src):
                dve.wait_ge(acc_loaded, 16 * (b + 1))
                for tt in tiles:
                    dve.wait_ge(proj_full, TT * n + tt + 1)
                    nc.vector.tensor_tensor(attn_acc[:, tt, :], src[:, (tt % 2) * N:(tt % 2 + 1) * N],
                                            attn_acc[:, tt, :], ALU.add).then_inc(proj_added, 1)

            def fc2_add(m, tt, half):
                dve.wait_ge(fc2_full, TT * m + tt + 1)
                nc.vector.tensor_tensor(mlp_acc[:, tt, :], tail[:, half * N:(half + 1) * N], mlp_acc[:, tt, :],
                                        ALU.add).then_inc(fc2_added, 1)

            def mask_q_or_k(n, i, dst, ready):
                for half in range(HALVES):
                    cols = slice(half * N, (half + 1) * N)
                    dve.wait_ge(qkv_full, 2 * HALVES * n + HALVES * i + half + 1)
                    nc.vector.scalar_tensor_tensor(out=dst[:, cols], in0=pair[i][:, cols],
                                                   scalar=w_qkv[:, QKV_W + i:QKV_W + i + 1], in1=mask_u8[:, cols],
                                                   op0=ALU.add, op1=ALU.mult).then_inc(ready, 1)

            def step(n, g, m, b, ln1=None, ln2=None, fin=None):
                if m is not None:
                    fc1_high(m)
                if ln2 is not None:
                    dve.wait_ge(x_again, 32 * b)
                    dve.wait_ge(proj_added, TT * G * b)
                    gate_sum(attn_acc, gate1, x1_gated, 0)
                dve.wait_ge(wq_scaled, 2 * n + 2)
                mask_q_or_k(n, 0, qf, q_full_ready)
                if ln2 is not None:
                    x1_and_statistics(ln2, 0)
                    pick_mod(1, ln2)
                    normalize(1, ln2, attn_acc, 0)
                    gate_sum(attn_acc, gate1, x1_gated, 1)
                    x1_and_statistics(ln2, 1)
                if ln1 is not None:
                    dve.wait_ge(x_loaded, 16 * ln1 + 16)
                    statistics(0)
                    dve.wait_ge(norm_step[0], 3 * ln1 + 1)
                    pick_mod(0, ln1)
                mask_q_or_k(n, 1, kf, k_full_ready)
                if ln1 is not None:
                    normalize(0, ln1, x_next)
                if ln2 is not None:
                    normalize(1, ln2, attn_acc, 1)
                dve.wait_ge(v_t, n + 1)
                nc.vector.tensor_copy(v_tok[:, :, :].rearrange("p t c -> p (t c)"), pair[2][:, :]).then_inc(v_ready, 1)
                if ln2 is not None:
                    evacuate2(ln2)
                if known(n, 0):
                    dve.wait_ge(ada_done, 3)
                    gate_row(0)
                    dve.wait_ge(ada_done, 6)
                    gate_row(1)
                    modulation(1)
                if ln1 is not None:
                    dve.wait_ge(mod_ready[0], ln1 + 1)
                    if m is None:
                        for t in range(1, TT, 2):
                            evacuate1(ln1, t)
                if m is not None:
                    for h in range(HG):
                        dve.wait_ge(stack_loaded[h], 16 * 6 * (n + 1))
                    u_high(m, ln1)
                    dve.wait_ge(mlp_acc_loaded, 16 * b)
                due = fillers(m is not None)[1]
                for t in range(TILES):
                    for what, tt in due.get(t, ()):
                        if what == "fc2":
                            fc2_add(m, tt, fc2_half(tt))
                    dve.wait_ge(score_full, TILES * n + t + 1)
                    nc.vector.tensor_reduce(neg_max[:, t:t + 1], pair[t % 3][:, :], AX_X, ALU.max,
                                            negate=True).then_inc(neg_max_ready, 1)
                dve.wait_ge(neg_max_ready, TILES * (n + 1))
                nc.vector.tensor_copy(stat[:, 0:TILES].bitcast(F32R), neg_max[:, :]).then_inc(stat_step, 1)
                dve.wait_ge(stat_step, 3 * n + 1)
                nc.vector.tensor_tensor(stat[:, TILES:2 * TILES], neg_max[:, :], stat[:, 0:TILES], ALU.subtract)
                dve.wait_ge(exp_done, 2 * TILES * n + TILES)
                nc.vector.reciprocal(inv_den[:, :], den[:, :]).then_inc(stat_step, 1)
                dve.wait_ge(stat_step, 3 * n + 2)
                nc.vector.tensor_copy(stat[:, 2 * TILES:3 * TILES].bitcast(F32R), inv_den[:, :]).then_inc(stat_step, 1)
                dve.wait_ge(stat_step, 3 * n + 3)
                nc.vector.tensor_tensor(stat[:, 3 * TILES:4 * TILES], inv_den[:, :], stat[:, 2 * TILES:3 * TILES],
                                        ALU.subtract).then_inc(stat_ready, 1)
                if m is not None:
                    for tt in range(FC2_INSIDE, TT - 2):
                        fc2_add(m, tt, fc2_half(tt))
                dve.wait_ge(stat_turned, n + 1)
                nc.vector.tensor_copy(stat_t[:, :], pair[2][:, 0:P]).then_inc(stat_t_ready, 1)
                if m is not None:
                    fc2_add(m, TT - 2, 0)
                    fc2_add(m, TT - 1, 1)
                scale_q_weights(n + 1)
                if fin is not None:
                    dve.wait_ge(x1_again, 32 * b)
                    dve.wait_ge(fc2_added, TT * G * b)
                    gate_sum(mlp_acc, gate2, mlp_gated)
                units = key_major_units(not known(g, 0))
                dve.wait_ge(den_spread, n + 1)
                nc.vector.tensor_copy(den_bc[:, :], place(units, "spread", 0)[:, :]).then_inc(den_bc_ready, 1)
                if fin is not None:
                    dve.wait_ge(mlp_gated, b)
                    add_residual(mlp_acc, None, 0)
                for j in range(TT // 2):
                    if ("proj", j) in units:
                        add_projection((2 * j, 2 * j + 1), n - 1, b, place(units, "proj", j))
                    if j == 0 and fin is not None:
                        add_residual(mlp_acc, final_ready, 1)
                dve.wait_ge(den_bc_ready, n + 1)
                for half in range(HALVES):
                    cols = slice(half * N, (half + 1) * N)
                    dve.wait_ge(probs_used, HALVES * TT * n + HALVES * (TT - 1) + half + 1)
                    nc.vector.tensor_tensor(attn_ch[:, cols], tail[:, cols], den_bc[:, cols], ALU.mult).then_inc(attn_ready, 1)
                if known(g, G - 1):
                    for j in range(TT // 2):
                        add_projection((2 * j, 2 * j + 1), n, b, pair[PROJ_PAIR[j]])

            loops(dve, step)
            fc1_high((B - 1) * G)
            dve.wait_ge(x_again, 32 * B)
            dve.wait_ge(proj_added, TT * G * B)
            pick_mod(1, B - 1)
            for part in range(2):
                gate_sum(attn_acc, gate1, x1_gated, part)
                x1_and_statistics(B - 1, part)
                normalize(1, B - 1, attn_acc, part)
            dve.wait_ge(mod_ready[1], B)
            evacuate2(B - 1)
            with dve.Fori(0, G - 1) as g:
                m = g + (B - 1) * G
                u_high(m)
                dve.wait_ge(fc1_full, JT * HALVES * (m + 1))
                fc1_high(m + 1)
                for tt in range(TT):
                    fc2_add(m, tt, tt % 2)
            u_high(B * G - 1)
            dve.wait_ge(x1_again, 32 * (B - 1) + 16)
            for tt in range(TT):
                fc2_add(B * G - 1, tt, tt % 2)
                dve.wait_ge(fc2_added, TT * (B * G - 1) + tt + 1)
                nc.vector.tensor_tensor(mlp_acc[:, tt, :], mlp_acc[:, tt, :], gate2[:, :], ALU.mult).then_inc(mlp_gated, 1)
                dve.wait_ge(mlp_gated, B + tt)
                nc.vector.tensor_tensor(x_next[:, tt, :], x_next[:, tt, :], mlp_acc[:, tt, :], ALU.add).then_inc(final_ready, 1)

        @block.tensor
        def _(pe):
            pe.wait_ge(silu_ready, 1)
            sl = silu[:, :].rearrange("p (k b) -> p k b", b=B)

            def modulate_chunk(i):
                pe.wait_ge(ada_loaded[i], 16)
                if i in (2, 5):
                    dst = tail[0:B, N:2 * N] if i == 2 else pair[1][0:B, 0:N]
                    for k in range(KT):
                        last = nc.tensor.matmul(dst, sl[:, k, :], ada_w[:, i % 4, k, :], start=k == 0, stop=k == KT - 1)
                else:
                    for f in range(KT):
                        col = ((i if i < 2 else i - 1) * KT + f) * B
                        for k in range(KT):
                            last = nc.tensor.matmul(tail[:, col:col + B], ada_w[:, i % 4, k, f * P:(f + 1) * P], sl[:, k, :],
                                                    start=k == 0, stop=k == KT - 1)
                last.then_inc(ada_done, 1)

            def transpose_tile(which, b, t):
                src = x_next if which == 0 else attn_acc
                dst, o = norm_place(which, t)
                pe.wait_ge(norm_ready[which], TT * b + t + 1)
                if which == 0 and t >= 4:
                    out_sem = odd_out if t % 2 else even_out
                    pe.wait_ge(out_sem[which], TT // 2 * b + t // 2 - 1)
                for k in range(KT):
                    last = nc.tensor.transpose(dst[:, o + k * P:o + (k + 1) * P], src[:, t, k * P:(k + 1) * P], ident[:, :])
                last.then_inc(norm_t[which], 1)

            def fc1(m, i, out=tail):
                j, half = i % JT, i // JT
                if i >= 2:
                    pe.wait_ge(gelu_ready, JT * HALVES * m + i - 1)
                dst = out[:, (i % 2) * N:(i % 2 + 1) * N]
                for a, (w, h) in enumerate(((w_lo, h2_hi), (w_hi, h2_lo), (w_hi, h2_hi))):
                    for k in range(KT):
                        last = nc.tensor.matmul(dst, w[:, (k * JT + j) * P:(k * JT + j + 1) * P], h[:, k, half * N:(half + 1) * N],
                                                start=a == 0 and k == 0, stop=a == 2 and k == KT - 1)
                last.then_inc(fc1_full, 1)

            def fc2_piece(m, tt, term):
                if term == 0:
                    if tt == 0:
                        pe.wait_ge(gelu_ready, JT * HALVES * (m + 1))
                    elif tt <= 2:
                        pe.wait_ge(fc2_added, TT * m + tt)
                    elif tt != 3:
                        pe.wait_ge(fc2_added, TT * m + tt - 1)
                    if tt == 0:
                        pe.wait_ge(u_ready, JT * HALVES * m + JT)
                        pe.wait_ge(w_hi_ready, 2 * m + 2)
                    if tt == TT // 2:
                        pe.wait_ge(u_ready, JT * HALVES * (m + 1))
                if tt == 0 and term == 2:
                    pe.wait_ge(w_ready, 2 * m + 2)
                fc2_term(tt, term, *((u_lo, w_hi), (u_hi, w_hi), (u_hi, w_lo))[term], fc2_half(tt))

            def v_piece(n, half, k):
                if k == 0:
                    pe.wait_ge(wqkv_loaded, 16 * (n + 1))
                    if half:
                        pe.wait_ge(v_ch_ready, HALVES * n + 1)
                last = nc.tensor.matmul(tail[:, N:2 * N], w_qkv[:, (2 * KT + k) * P:(2 * KT + k + 1) * P],
                                        h1[:, k, half * N:(half + 1) * N], start=k == 0, stop=k == KT - 1)
                if k == KT - 1:
                    last.then_inc(v_full, 1)

            def fc2_term(tt, term, u, w, half):
                for j in range(JT):
                    last = nc.tensor.matmul(tail[:, half * N:(half + 1) * N], u[:, j, tt * P:(tt + 1) * P],
                                            w[:, j * C:(j + 1) * C], start=term == 0 and j == 0, stop=term == 2 and j == JT - 1)
                if term == 2:
                    last.then_inc(fc2_full, 1)

            def fc2(m, tt):
                for term in range(3):
                    fc2_piece(m, tt, term)

            def fc2_alone(m):
                pe.wait_ge(fc2_added, TT * m)
                pe.wait_ge(w_ready, 2 * m + 2)
                pe.wait_ge(u_hi_ready, JT * HALVES * (m + 1))
                for tt in range(TT):
                    if tt >= 2:
                        pe.wait_ge(fc2_added, TT * m + tt - 1)
                    fc2_term(tt, 0, u_hi, w2_hi, tt % 2)
                    fc2_term(tt, 1, u_hi, w2_lo, tt % 2)
                    if tt == 0:
                        pe.wait_ge(u_ready, JT * HALVES * (m + 1))
                    fc2_term(tt, 2, u_lo, w2_hi, tt % 2)

            def project(n, tiles, dst):
                for tt in tiles:
                    pe.wait_ge(attn_ready, HALVES * n + tt // (TT // HALVES) + 1)
                    nc.tensor.matmul(dst[:, (tt % 2) * N:(tt % 2 + 1) * N], attn_ch[:, tt * P:(tt + 1) * P],
                                     w_proj[:, :], start=True, stop=True).then_inc(proj_full, 1)

            modulate_chunk(0)
            modulate_chunk(1)
            pe.wait_ge(consts_ready, 2)
            for t in range(TT):
                transpose_tile(0, 0, t)
            pe.wait_ge(even_out[0], TT // 2)
            pe.wait_ge(odd_out[0], TT // 2)
            for half in range(HALVES):
                for k in range(KT):
                    v_piece(0, half, k)

            def step(n, g, m, b, ln1=None, ln2=None, fin=None):
                pe.wait_ge(wq_scaled, 2 * n + 2)
                pe.wait_ge(even_out[0], TT // 2 * (b + 1))
                pe.wait_ge(odd_out[0], TT // 2 * (b + 1))
                for i in range(2):
                    if i == 1 and ln2 is not None:
                        pe.wait_ge(proj_added, TT * G * b)
                    for half in range(HALVES):
                        for k in range(KT):
                            last = nc.tensor.matmul(pair[i][:, half * N:(half + 1) * N], w_qkv[:, (i * KT + k) * P:(i * KT + k + 1) * P],
                                                    h1[:, k, half * N:(half + 1) * N], start=k == 0, stop=k == KT - 1)
                        last.then_inc(qkv_full, 1)
                pe.wait_ge(v_ch_ready, HALVES * (n + 1))
                for t in range(TT):
                    last = nc.tensor.transpose(pair[2][:, t * P:(t + 1) * P], v_ch[:, t * P:(t + 1) * P], ident[:, :])
                last.then_inc(v_t, 1)
                if ln2 is not None:
                    pe.wait_ge(attn_ready, HALVES * n)
                    pe.wait_ge(q_full_ready, HALVES * (n + 1))
                    for t in range(TT // 2):
                        transpose_tile(1, ln2, t)
                    pe.wait_ge(h2_ready, TT * ln2 + TT // 2)
                if m is not None:
                    pe.wait_ge(w_ready, 2 * m + 1)
                    pe.wait_ge(attn_ready, HALVES * n)
                    fc1(m, 0)
                if known(n, 0):
                    pe.wait_ge(mod_step, 2)
                    pe.wait_ge(v_ch_ready, HALVES)
                    pe.wait_ge(k_full_ready, HALVES)
                    for i in range(2, 6):
                        modulate_chunk(i)
                    pe.wait_ge(mod_step, 4)
                    pe.wait_ge(gates_ready, 2)
                if m is not None:
                    for i in range(1, JT * HALVES):
                        if ln2 is not None and i == 1:
                            pe.wait_ge(k_full_ready, HALVES * (n + 1))
                            pe.wait_ge(v_ready, n + 1)
                            for t in range(TT // 2, TT):
                                transpose_tile(1, ln2, t)
                        if ln2 is not None and i == JT:
                            pe.wait_ge(h2_ready, TT * b)
                        fc1(m, i)
                        if ln1 is not None:
                            if i == 1:
                                pe.wait_ge(k_full_ready, HALVES * (n + 1))
                                pe.wait_ge(v_ready, n + 1)
                            transpose_tile(0, ln1, i - 1)
                    if ln1 is not None:
                        transpose_tile(0, ln1, TT - 1)
                elif ln1 is not None:
                    pe.wait_ge(k_full_ready, HALVES * (n + 1))
                    pe.wait_ge(v_ready, n + 1)
                    for t in range(TT):
                        transpose_tile(0, ln1, t)
                for which, ln in ((0, ln1), (1, ln2)):
                    if ln is not None:
                        pe.wait_ge(even_out[which], TT // 2 * ln + TT // 2)
                        pe.wait_ge(odd_out[which], TT // 2 * ln + TT // 2)
                pe.wait_ge(mask_rows, 2 * (b + 1))
                pe.wait_ge(q_full_ready, HALVES * (n + 1))
                pe.wait_ge(k_full_ready, HALVES * (n + 1))
                pe.wait_ge(v_ready, n + 1)
                more = not (known(b, B - 1) and known(g, G - 1))
                at = fillers(m is not None)[0]
                if m is None and not known(g, 0):
                    pe.wait_ge(attn_ready, HALVES * n)
                for t in range(TILES):
                    h, qt = t // TT, t % TT
                    for what, i, piece in at.get(t, ()):
                        if what == "fc2":
                            if i == 3 and piece == 0 and more:
                                pe.wait_ge(v_ch_ready, HALVES * (n + 2))
                            fc2_piece(m, i, piece)
                        elif more:
                            v_piece(n + 1, i, piece)
                    if qt == 0:
                        pe.wait_ge(stack_loaded[h], 16 * 6 * (n + 1))
                    if t >= 3:
                        pe.wait_ge(exp_done, 2 * TILES * n + t - 2)
                    for half in range(HALVES):
                        last = nc.tensor.matmul(pair[t % 3][:, half * N:(half + 1) * N], q_st[0:MAX_ROW, h, qt * P:(qt + 1) * P],
                                                k_st[0:MAX_ROW, h, half * N:(half + 1) * N], start=True, stop=True)
                    last.then_inc(score_full, 1)
                if m is not None:
                    for tt in range(FC2_INSIDE, TT - 2):
                        fc2(m, tt)
                pe.wait_ge(stat_ready, n + 1)
                nc.tensor.transpose(pair[2][:, 0:P], stat[:, :], ident[:, :]).then_inc(stat_turned, 1)
                if m is not None:
                    fc2(m, TT - 2)
                    fc2(m, TT - 1)
                pe.wait_ge(rows_loaded, 16 * (n + 1))
                pe.wait_ge(stat_t_ready, n + 1)

                def weigh(kt, half):
                    if half == 0:
                        pe.wait_ge(exp_done, 2 * TILES * n + TILES + HG * (kt + 1))
                    for h in range(HG):
                        last = nc.tensor.matmul(tail[h * HD:(h + 1) * HD, half * N:(half + 1) * N],
                                                v_tok[:, kt, h * HD:(h + 1) * HD],
                                                probs[:, (kt % 2) * HG + h, half * N:(half + 1) * N],
                                                start=kt == 0, stop=kt == TT - 1)
                    last.then_inc(probs_used, 1)

                if m is not None:
                    pe.wait_ge(fc2_added, TT * (m + 1))
                else:
                    pe.wait_ge(v_ch_ready, HALVES * (n + 2))
                units = key_major_units(not known(g, 0))
                for p, (what, i) in enumerate(units):
                    if p >= 3:
                        before, prev = units[p - 3]
                        if before == "score":
                            pe.wait_ge(exp_done, 2 * TILES * n + TILES + prev + 1)
                        elif before == "spread":
                            pe.wait_ge(den_bc_ready, n + 1)
                        else:
                            pe.wait_ge(proj_added, TT * n - TT + 2 * prev + 2)
                    dst = pair[p % 3]
                    if what == "score":
                        kt, h = i // HG, i % HG
                        for half in range(HALVES):
                            last = nc.tensor.matmul(dst[:, half * N:(half + 1) * N], k_st[0:MAX_ROW + 2, h, kt * P:(kt + 1) * P],
                                                    q_st[0:MAX_ROW + 2, h, half * N:(half + 1) * N], start=True, stop=True)
                        last.then_inc(score_t_full, 1)
                        if h in WEIGH_AFTER and kt:
                            weigh(kt - 1, WEIGH_AFTER.index(h))
                    elif what == "spread":
                        pe.wait_ge(den_loaded, 16 * (n + 1))
                        for half in range(HALVES):
                            last = nc.tensor.matmul(dst[:, half * N:(half + 1) * N], head_sel[:, :], den_row[:, half * N:(half + 1) * N],
                                                    start=True, stop=True)
                        last.then_inc(den_spread, 1)
                    else:
                        if i == 0:
                            pe.wait_ge(wproj_loaded, 16 * n)
                        project(n - 1, (2 * i, 2 * i + 1), dst)
                for half in range(HALVES):
                    weigh(TT - 1, half)
                if known(g, G - 1):
                    pe.wait_ge(wproj_loaded, 16 * (n + 1))
                    for i in range(TT // 2):
                        if i == 3:
                            pe.wait_ge(proj_added, TT * n + 2 * 2)
                        project(n, (2 * i, 2 * i + 1), pair[PROJ_PAIR[i]])

            loops(pe, step)
            pe.wait_ge(proj_added, TT * G * B)
            for t in range(TT):
                transpose_tile(1, B - 1, t)

            def fc1_alone(m, tiles):
                for i in tiles:
                    fc1(m, i, pair[0])

            m = (B - 1) * G
            pe.wait_ge(w_ready, 2 * m + 1)
            pe.wait_ge(h2_ready, TT * (B - 1) + TT // 2)
            fc1_alone(m, range(JT))
            pe.wait_ge(h2_ready, TT * B)
            fc1_alone(m, range(JT, JT * HALVES))
            fc2_alone(m)
            with pe.Fori(1, G) as g:
                m = g + (B - 1) * G
                pe.wait_ge(w_ready, 2 * m + 1)
                fc1_alone(m, range(JT * HALVES))
                fc2_alone(m)


def kernel(x, cond_1024, mask_BxS_bk1, L0_cond_qkv_w, L0_cond_qkv_b, L0_cond_proj_w, L0_cond_proj_b,
           L0_cond_fc1_w, L0_cond_fc1_b, L0_cond_fc2_w, L0_cond_fc2_b, L0_cond_ada_w, L0_cond_ada_b):
    import numpy as np
    import concourse.bacc as bacc
    from concourse.bass_utils import run_bass_kernel_spmd

    def rows(a):
        return np.ascontiguousarray(a)

    def wrapped(a):
        return np.concatenate([a, a[:1]], axis=0)

    qkv = np.asarray(L0_cond_qkv_w).reshape(3, G, P, KT, P).transpose(1, 4, 0, 3, 2).reshape(G, P, QKV_W)
    qkv_b = np.asarray(L0_cond_qkv_b).reshape(3, G, P).transpose(1, 2, 0)
    fc1 = np.asarray(L0_cond_fc1_w).reshape(G, JT * P, KT, P).transpose(0, 3, 2, 1).reshape(G, P, FC1_W)
    fc1_b = np.asarray(L0_cond_fc1_b).reshape(G, JT, P).transpose(0, 2, 1)
    fc2 = np.asarray(L0_cond_fc2_w).reshape(C, G, JT, P).transpose(1, 3, 2, 0).reshape(G, P, FC2_W)
    ada = np.asarray(L0_cond_ada_w).reshape(6, C, KT, P).transpose(0, 3, 2, 1)
    ada_b = np.asarray(L0_cond_ada_b).reshape(6, KT, P)
    arrays = {
        "x": rows(x),
        "cond_t": rows(np.asarray(cond_1024).reshape(B, KT, P).transpose(2, 1, 0).reshape(P, KT * B)),
        "mask": rows(mask_BxS_bk1),
        "wqkv": rows(wrapped(np.concatenate([qkv, qkv_b], axis=2))),
        "wproj": rows(np.asarray(L0_cond_proj_w).T.reshape(G, P, C)),
        "wfc1": rows(wrapped(np.concatenate([fc1, fc1_b], axis=2))),
        "wfc2": rows(fc2),
        "proj_b": rows(np.asarray(L0_cond_proj_b).reshape(1, 1, C)),
        "fc2_b": rows(np.asarray(L0_cond_fc2_b).reshape(1, 1, C)),
        "ada_wt": rows(ada),
        "ada_bt": rows(ada_b[[0, 1, 3, 4]].transpose(2, 0, 1).reshape(P, NMOD)),
        "ada_bg": rows(ada_b[[2, 5]].reshape(1, 2 * C)),
    }
    nc = bacc.Bacc("TRN2", target_bir_lowering=False, num_devices=1, dynamic_dma_scratch_size=1024)
    args = [nc.dram_tensor(f"in_{n}", a.shape, mybir.dt.from_np(a.dtype), kind="ExternalInput").ap() for n, a in arrays.items()]
    out = nc.dram_tensor("out_x", (B, S, C), F32, kind="ExternalOutput").ap()
    block_kernel(nc, *args, out)
    r = run_bass_kernel_spmd(nc, [{f"in_{n}": a for n, a in arrays.items()}], core_ids=[0])
    return r.results[0]["out_x"]
```
